# Optimizing a Trainium2 kernel written in Bass

```python
import numpy as np
import jax
import jax.numpy as jnp

def _softmax(x, axis=-1):
    return jax.nn.softmax(x, axis=axis)

def _gelu(x):
    return jax.nn.gelu(x, approximate=True)

def _silu(x):
    return jax.nn.silu(x)

def _sigmoid(x):
    return jax.nn.sigmoid(x)

def _layernorm(x, axis=-1, eps=1e-05):
    m = jnp.mean(x, axis=axis, keepdims=True)
    v = jnp.var(x, axis=axis, keepdims=True)
    return (x - m) / jnp.sqrt(v + eps)

def _scatter_add(tgt, idx, src, axis=0):
    return tgt.at[idx].add(src)

def _segment_sum(src, seg, n):
    return jax.ops.segment_sum(src, seg, n)
kernel_name = 'mk_gnn_preln_d1_gnn_r8_cd0185'

def setup_inputs(seed: int=0):
    np.random.seed(seed)
    _w = jnp.asarray

    def _rec_inputs():
        import jax
        import jax.numpy as jnp
        _gk = jax.random.key(seed)
        x = -0.0003713 + 1 * jax.random.normal(jax.random.fold_in(_gk, 1), (12500, 128), jnp.float32)
        src = jax.random.randint(jax.random.fold_in(_gk, 2), (200000,), 0, 12500, jnp.int32)
        dst = jax.random.randint(jax.random.fold_in(_gk, 3), (200000,), 0, 12500, jnp.int32)
        _o = jnp.argsort(dst, stable=True)
        src = src[_o]
        dst = dst[_o]
        edge_attr_128 = 5.93493e-05 + 1.00006 * jax.random.normal(jax.random.fold_in(_gk, 11), (200000, 128), jnp.float32)
        return (x, src, dst, edge_attr_128)
    x, src, dst, edge_attr_128 = _rec_inputs()

    def _L0_gnn_setup():
        import jax, jax.numpy as jnp
        import numpy as np
        N_NODES = 12500
        N_EDGES = 75000
        D_NODE = 128
        D_EDGE = 128
        HIDDEN = 128
        LN_EPS = 1e-05
        key = jax.random.key(seed)
        ks = jax.random.split(key, 12)
        x = jax.random.normal(ks[0], (N_NODES, D_NODE), dtype=jnp.float32)
        edge_index = jax.random.randint(ks[1], (2, N_EDGES), 0, N_NODES, dtype=jnp.int64)
        edge_attr = jax.random.normal(ks[2], (N_EDGES, D_EDGE), dtype=jnp.float32)
        in_dim = D_NODE + D_EDGE
        s1 = 1.0 / np.sqrt(in_dim)
        s2 = 1.0 / np.sqrt(HIDDEN)
        W1 = jax.random.uniform(ks[3], (in_dim, HIDDEN), minval=-s1, maxval=s1, dtype=jnp.float32)
        b1 = jax.random.uniform(ks[4], (HIDDEN,), minval=-s1, maxval=s1, dtype=jnp.float32)
        W2 = jax.random.uniform(ks[5], (HIDDEN, HIDDEN), minval=-s2, maxval=s2, dtype=jnp.float32)
        b2 = jax.random.uniform(ks[6], (HIDDEN,), minval=-s2, maxval=s2, dtype=jnp.float32)
        W3 = jax.random.uniform(ks[7], (HIDDEN, D_NODE), minval=-s2, maxval=s2, dtype=jnp.float32)
        b3 = jax.random.uniform(ks[8], (D_NODE,), minval=-s2, maxval=s2, dtype=jnp.float32)
        ln_w = jnp.ones((D_NODE,), dtype=jnp.float32)
        ln_b = jnp.zeros((D_NODE,), dtype=jnp.float32)
        return {'x': x, 'edge_index': edge_index, 'edge_attr': edge_attr, 'W1': W1, 'b1': b1, 'W2': W2, 'b2': b2, 'W3': W3, 'b3': b3, 'ln_w': ln_w, 'ln_b': ln_b}
    _L0_gnn_all = _L0_gnn_setup()
    _L0_gnn_in = {k: v for k, v in _L0_gnn_all.items() if k in ('W1', 'b1', 'W2', 'b2', 'W3', 'b3', 'ln_w', 'ln_b')}
    del _L0_gnn_all
    return {'x': x, 'src': src, 'dst': dst, 'edge_attr_128': edge_attr_128, 'L0_gnn_W1': _L0_gnn_in['W1'], 'L0_gnn_b1': _L0_gnn_in['b1'], 'L0_gnn_W2': _L0_gnn_in['W2'], 'L0_gnn_b2': _L0_gnn_in['b2'], 'L0_gnn_W3': _L0_gnn_in['W3'], 'L0_gnn_b3': _L0_gnn_in['b3'], 'L0_gnn_ln_w': _L0_gnn_in['ln_w'], 'L0_gnn_ln_b': _L0_gnn_in['ln_b']}

def reference(x, src, dst, edge_attr_128, L0_gnn_W1, L0_gnn_b1, L0_gnn_W2, L0_gnn_b2, L0_gnn_W3, L0_gnn_b3, L0_gnn_ln_w, L0_gnn_ln_b):
    import jax
    import jax.numpy as jnp

    def _L0_gnn_ref(x, edge_index, edge_attr, W1, b1, W2, b2, W3, b3, ln_w, ln_b):
        import jax, jax.numpy as jnp
        import numpy as np
        N_NODES = 12500
        N_EDGES = 75000
        D_NODE = 128
        D_EDGE = 128
        HIDDEN = 128
        LN_EPS = 1e-05
        col = edge_index[1]
        agg = jax.ops.segment_sum(edge_attr, col, num_segments=x.shape[0])
        h = jnp.concatenate([x, agg], axis=-1)
        h = jax.nn.relu(h @ W1 + b1)
        h = jax.nn.relu(h @ W2 + b2)
        h = h @ W3 + b3
        mu = jnp.mean(h, axis=-1, keepdims=True)
        var = jnp.mean(jnp.square(h - mu), axis=-1, keepdims=True)
        h = (h - mu) * jax.lax.rsqrt(var + LN_EPS) * ln_w + ln_b
        return h
    edge_index = jnp.stack([src, dst])
    h = jnp.maximum(_layernorm(x, axis=-1), 0.0)
    x = x + _L0_gnn_ref(h, edge_index, edge_attr_128, L0_gnn_W1, L0_gnn_b1, L0_gnn_W2, L0_gnn_b2, L0_gnn_W3, L0_gnn_b3, L0_gnn_ln_w, L0_gnn_ln_b)
    return x

_drawn_inputs = setup_inputs


def setup_inputs(seed=0):
    import zlib

    import numpy as np

    out = dict(_drawn_inputs(seed))
    spreads = {'L0_gnn_ln_w': (1.0, 0.2), 'L0_gnn_ln_b': (0.0, 0.1)}
    factors = {'L0_gnn_b1': 3.368}
    for name, (base, spread) in spreads.items():
        noise = np.random.default_rng([zlib.crc32(name.encode()), seed]).standard_normal(out[name].shape)
        drawn = base * np.exp(spread * noise) if base else spread * noise
        out[name] = jnp.asarray(drawn.astype(out[name].dtype))
    for name, factor in factors.items():
        out[name] = (out[name] * factor).astype(out[name].dtype)
    return out
```

```python
from contextlib import ExitStack

import numpy as np

import concourse.bass as bass
from concourse import mybir

F32 = mybir.dt.float32
I32 = mybir.dt.int32
ALU = mybir.AluOpType
ACT = mybir.ActivationFunctionType
AX = mybir.AxisListType

P = 128
NODES, EDGES, D = 12500, 200000, 128
EPS = 1e-5

PER = 3
CHUNK = P * PER
WIN = 32
QC = P // WIN
QUAD = QC * CHUNK
QUADS = EDGES // QUAD
CHUNKS = QUADS * QC
TAIL0 = EDGES - CHUNK
DONE = CHUNKS * CHUNK - TAIL0
OCT = 2 * QC
GROUPS = NODES // CHUNK
LAST0 = NODES - CHUNK
ROWT = -(-(CHUNKS + 1) // P)
LROW = CHUNKS - (ROWT - 1) * P
NCOL = ROWT * P
RING = 8
SLACK = 96
NODES_PER_CHUNK = 24
BANK = 512
WINDOWS = -(-NODES // BANK)
AGG = WINDOWS * BANK
BLOCK = 12
BLOCKS = EDGES // (P * BLOCK)
REST = EDGES - BLOCKS * P * BLOCK
RP = 64
RC = REST // RP
TRIPLES = BLOCKS * BLOCK // 3 + 2
XAHEAD = 3
AHEAD = 6
HALVES = GROUPS - 1


def gnn_kernel(nc, x, dst, edges, w1, b1, w2, b2, w3, b3, lnw, lnb, out):
    assert GROUPS == 32 and QUADS == 4 * HALVES + AHEAD and RC * RP == REST
    with ExitStack() as ctx:
        def sb(name, shape, dt=F32):
            return ctx.enter_context(nc.sbuf_tensor(name, shape, dt))

        def sem(name):
            return ctx.enter_context(nc.semaphore(name))

        ring = sb("ring", [P, RING, QC * PER * D])
        agg = sb("agg", [P, AGG])
        xs = sb("xs", [P, (GROUPS + 1) * CHUNK])
        dst_i = sb("dst_i", [P, ROWT, CHUNK], I32)
        local = sb("local", [P, ROWT * CHUNK])
        local3 = local[:, :].rearrange("p (t k) -> p t k", t=ROWT)
        local_t = sb("local_t", [P, PER, NCOL])
        onehot = sb("onehot", [P, 2, OCT, PER, WIN])
        part = sb("part", [P, 2, D])
        place = sb("place", [P, 2, P])
        iota = sb("iota", [P, BANK])
        ident = sb("ident", [P, P])
        pidx = sb("pidx", [P, 1])
        widx = sb("widx", [P, 1])
        least = sb("least", [P, ROWT])
        turn = sb("turn", [P, ROWT])
        span = sb("span", [P, ROWT])
        least_row = sb("least_row", [1, NCOL])
        base_i = sb("base_i", [1, 3 + QUADS + 1 + 2], I32)
        row_at = sb("row_at", [P, QUADS + 1])
        rows_at = sb("rows_at", [P, AHEAD])
        excess = sb("excess", [P, 5])
        excess1 = sb("excess1", [P, 1])
        worst = sb("worst", [1, 1])
        flag_i = sb("flag_i", [1, 1], I32)
        signs = sb("signs", [1, 2, P])
        eps = sb("eps", [P, 1])
        w1x = sb("w1x", [P, P])
        w1a = sb("w1a", [P, P])
        w2s = sb("w2s", [P, P])
        w3s = sb("w3s", [P, P])
        b1s = sb("b1s", [P, 1])
        b2s = sb("b2s", [P, 1])
        b3s = sb("b3s", [P, D])
        lnws = sb("lnws", [P, D])
        lnbs = sb("lnbs", [P, D])
        x_stats = sb("x_stats", [P, PER, 6])
        x_mv = sb("x_mv", [P, PER, 2])
        x_std = sb("x_std", [P, PER])
        x_rstd = sb("x_rstd", [P, PER])
        x_shift = sb("x_shift", [P, PER])
        h = sb("h", [P, PER, D])
        h_t = sb("h_t", [P, CHUNK])
        hid1 = sb("hid1", [P, CHUNK])
        hid2 = sb("hid2", [P, PER, P])
        y = sb("y", [P, PER, D])
        z = sb("z", [P, PER, D])
        y_stats = sb("y_stats", [P, PER, 6])
        y_mv = sb("y_mv", [P, PER, 2])
        y_std = sb("y_std", [P, PER])
        y_rstd = sb("y_rstd", [P, PER])

        def bank(name):
            return ctx.enter_context(nc.psum_tensor(name, [P, BANK], F32))

        part_ps = [bank("part_ps0"), bank("part_ps1")]
        place_ps = [bank("place_ps0"), bank("place_ps1")]
        ht_ps, hid1_ps, hid2_ps, y_ps = bank("ht_ps"), bank("hid1_ps"), bank("hid2_ps"), bank("y_ps")

        dst_padded = sem("dst_padded")
        dst_loaded = sem("dst_loaded")
        x_loaded = [sem("x_loaded_even"), sem("x_loaded_odd")]
        wts_loaded = sem("wts_loaded")
        iotas_ready = sem("iotas_ready")
        ident_ready = sem("ident_ready")
        agg_zeroed = sem("agg_zeroed")
        least_ready = sem("least_ready")
        local_ready = sem("local_ready")
        span_ready = sem("span_ready")
        least_t_done = sem("least_t_done")
        least_row_ready = sem("least_row_ready")
        local_t_done = sem("local_t_done")
        local_t_ready = sem("local_t_ready")
        tail_masked = sem("tail_masked")
        base_ready = sem("base_ready")
        row_at_done = sem("row_at_done")
        row_at_ready = sem("row_at_ready")
        excess_ready = sem("excess_ready")
        excess_t_done = sem("excess_t_done")
        worst_ready = sem("worst_ready")
        flag_ready = sem("flag_ready")
        edges_loaded = [sem(f"edges_loaded{k}") for k in range(RING)]
        onehot_ready = sem("onehot_ready")
        seg_done = sem("seg_done")
        part_copied = sem("part_copied")
        rows_ready = sem("rows_ready")
        place_ready = sem("place_ready")
        placed = sem("placed")
        added = sem("added")
        dve_went_on = sem("dve_went_on")
        pool_went_on = sem("pool_went_on")
        dst2_loaded = sem("dst2_loaded")
        dst2_ready = sem("dst2_ready")
        block_loaded = [sem("block_loaded0"), sem("block_loaded1")]
        rest_loaded = sem("rest_loaded")
        block_done = sem("block_done")
        dense_ready = sem("dense_ready")
        dense_used = sem("dense_used")
        zeros_ready = sem("zeros_ready")
        window_done = sem("window_done")
        window_free = sem("window_free")
        x_stats_done = sem("x_stats_done")
        x_mv_ready = sem("x_mv_ready")
        x_std_ready = sem("x_std_ready")
        x_rstd_done = sem("x_rstd_done")
        x_shift_ready = sem("x_shift_ready")
        h_ready = sem("h_ready")
        h_transposed = sem("h_transposed")
        ht_ready = sem("ht_ready")
        hid1_done = sem("hid1_done")
        hid1_ready = sem("hid1_ready")
        hid2_done = sem("hid2_done")
        hid2_ready = sem("hid2_ready")
        y_done = sem("y_done")
        y_evacuated = sem("y_evacuated")
        y_stats_done = sem("y_stats_done")
        y_mv_ready = sem("y_mv_ready")
        y_std_ready = sem("y_std_ready")
        y_rstd_done = sem("y_rstd_done")
        y_centered = sem("y_centered")
        x_biased = sem("x_biased")
        out_ready = sem("out_ready")
        stored = sem("stored")

        def quad_of_edges(q):
            return edges[bass.ds(q * QUAD, QUAD), :].rearrange("(s p j) f -> p s (j f)", p=P, j=PER)

        def ring_slot(k):
            return ring[:, k, :].rearrange("p (s e) -> p s e", s=QC)

        def group_rows(t, n0):
            return t[bass.ds(n0, CHUNK), :].rearrange("(p j) f -> p (j f)", j=PER)

        def xg(g, j=None):
            if j is None:
                return xs[:, bass.ds(g * CHUNK, CHUNK)]
            return xs[:, bass.ds(g * CHUNK + j * D, D)]

        def branch(eng, fast, general):
            eng.wait_ge(flag_ready, 1)
            fits = eng.value_load(flag_i[0:1, 0:1])
            with eng.If(fits != 0):
                fast()
            with eng.Else():
                general()

        with nc.Block() as block:

            @block.sync
            def _(sp):
                full = (ROWT - 1) * P
                sp.dma_start(dst_i[:, 0:ROWT - 1, :],
                             dst[0:full * CHUNK].rearrange("(t p k) -> p t k", p=P, k=CHUNK)).then_inc(dst_loaded, 16)
                sp.wait_ge(dst_padded, 1)
                sp.dma_start(dst_i[0:LROW, ROWT - 1, :],
                             dst[full * CHUNK:CHUNKS * CHUNK].rearrange("(p k) -> p k", k=CHUNK)).then_inc(dst_loaded, 16)
                sp.dma_start(dst_i[LROW:LROW + 1, ROWT - 1, :],
                             dst[TAIL0:EDGES].rearrange("(p k) -> p k", k=CHUNK)).then_inc(dst_loaded, 16)

                def load_x(g, par, before):
                    if not (isinstance(before, int) and before == 0):
                        sp.wait_ge(x_loaded[par], 16 * before)
                    sp.dma_start(xg(g), group_rows(x, g * CHUNK)).then_inc(x_loaded[par], 16)

                def load_last_x():
                    sp.wait_ge(x_loaded[GROUPS % 2], 16 * (GROUPS // 2))
                    sp.dma_start(xg(GROUPS), group_rows(x, LAST0)).then_inc(x_loaded[GROUPS % 2], 16)

                load_x(0, 0, 0)
                load_x(1, 1, 0)
                for q in range(RING):
                    sp.dma_start(ring_slot(q), quad_of_edges(q)).then_inc(edges_loaded[q], 16)
                for g in range(2, XAHEAD):
                    load_x(g, g % 2, g // 2)

                def store(g):
                    sp.wait_ge(out_ready, g + 1)
                    sp.dma_start(group_rows(out, g * CHUNK), xg(g)).then_inc(stored, 16)

                def store_last():
                    sp.wait_ge(out_ready, GROUPS + 1)
                    sp.wait_ge(stored, 16 * GROUPS)
                    sp.dma_start(group_rows(out, LAST0), xg(GROUPS)).then_inc(stored, 16)
                    sp.wait_ge(stored, 16 * (GROUPS + 1))

                def reload(q, slot):
                    sp.wait_ge(seg_done, q - RING + 1)
                    sp.dma_start(ring_slot(slot), quad_of_edges(q)).then_inc(edges_loaded[slot], 16)

                def fast():
                    for q in range(RING, RING + AHEAD):
                        reload(q, q % RING)

                    def step(i, par, pairs):
                        load_x(i + XAHEAD, (par + XAHEAD) % 2, pairs + (par + XAHEAD) // 2)
                        for k in range(4):
                            reload(4 * i + RING + AHEAD + k, (4 * par + AHEAD + k) % RING)

                    step(0, 0, 0)
                    with sp.Fori(0, (HALVES - 3) // 2) as t:
                        step(2 * t + 1, 1, t)
                        store(2 * t)
                        step(2 * t + 2, 0, t + 1)
                        store(2 * t + 1)
                    load_last_x()
                    sp.wait_ge(seg_done, QUADS - RING + 1)
                    tail = QUADS % RING
                    sp.dma_start(ring[:, tail, 0:PER * D],
                                 edges[TAIL0:EDGES, :].rearrange("(p j) f -> p (j f)", j=PER)).then_inc(edges_loaded[tail], 16)
                    for g in range(HALVES - 3, GROUPS):
                        store(g)
                    store_last()

                def general():
                    d2 = dst_i[:, :, :].rearrange("p t k -> p (t k)")
                    sp.dma_start(d2[:, 0:BLOCKS * BLOCK].rearrange("p (b c) -> p b c", c=BLOCK),
                                 dst[0:BLOCKS * P * BLOCK].rearrange("(b p c) -> p b c", p=P, c=BLOCK)
                                 ).then_inc(dst2_loaded, 16)
                    sp.dma_start(d2[0:RP, BLOCKS * BLOCK:BLOCKS * BLOCK + RC],
                                 dst[EDGES - REST:EDGES].rearrange("(p c) -> p c", c=RC)).then_inc(dst2_loaded, 16)
                    for k in range(RING):
                        sp.wait_ge(edges_loaded[k], 16)
                    sp.dma_start(ring[0:RP, 4, 0:RC * D],
                                 edges[EDGES - REST:EDGES, :].rearrange("(p c) f -> p (c f)", c=RC)).then_inc(rest_loaded, 16)
                    with sp.Fori(0, WINDOWS) as w:
                        with sp.Fori(0, BLOCKS // 2) as b:
                            for par in range(2):
                                sp.wait_ge(block_done, w * BLOCKS + 2 * b + par + 1)
                                sp.dma_start(ring[:, par, :],
                                             edges[bass.ds((2 * b + par) * P * BLOCK, P * BLOCK), :]
                                             .rearrange("(p c) f -> p (c f)", c=BLOCK)).then_inc(block_loaded[par], 16)
                    load_x(XAHEAD, XAHEAD % 2, XAHEAD // 2)
                    with sp.Fori(2, GROUPS // 2) as t:
                        load_x(2 * t, 0, t)
                        load_x(2 * t + 1, 1, t)
                    load_last_x()
                    with sp.Fori(0, GROUPS) as g:
                        store(g)
                    store_last()

                branch(sp, fast, general)

            @block.tensor
            def _(pe):
                pe.wait_ge(least_ready, 1)
                pe.wait_ge(ident_ready, 1)
                for t in range(ROWT):
                    row = part_ps[t // 4][0:1, (t % 4) * P:(t % 4 + 1) * P]
                    last = nc.tensor.matmul(row, least[:, t:t + 1], ident[:, :], start=True, stop=True)
                last.then_inc(least_t_done, 1)
                pe.wait_ge(local_ready, 1)
                banks = [ht_ps, hid1_ps, hid2_ps]
                for t in range(ROWT):
                    if t >= len(banks):
                        pe.wait_ge(local_t_ready, t - len(banks) + 1)
                    for j in range(PER):
                        last = nc.tensor.transpose(banks[t % 3][:, j * P:(j + 1) * P], local3[:, t, j::PER], ident[:, :])
                    last.then_inc(local_t_done, 1)
                pe.wait_ge(least_row_ready, 1)
                for s in range(QC):
                    o = place_ps[0][s * WIN:(s + 1) * WIN, 0:QUADS + 1]
                    nc.tensor.matmul(o, signs[0:1, 0, 0:WIN], least_row[0:1, s:s + 4 * QUADS + 1:QC], start=True, stop=False)
                    last = nc.tensor.matmul(o, signs[0:1, 1, 0:WIN], least_row[0:1, 0:4 * QUADS + 1:QC], start=False, stop=True)
                last.then_inc(row_at_done, 1)
                pe.wait_ge(excess_ready, 1)
                nc.tensor.matmul(place_ps[1][0:1, 0:P], excess1[:, 0:1], ident[:, :], start=True, stop=True).then_inc(excess_t_done, 1)

                def seg(q, par_q, load_count, oct_ready=None):
                    slot = par_q % RING
                    pe.wait_ge(edges_loaded[slot], load_count)
                    if oct_ready is not None:
                        pe.wait_ge(onehot_ready, oct_ready)
                    e = ring_slot(slot)
                    oct_par, first = (par_q // 2) % 2, (par_q % 2) * QC
                    for j in range(PER):
                        for s in range(QC):
                            last = nc.tensor.matmul(part_ps[par_q % 2][s * WIN:(s + 1) * WIN, 0:D],
                                                    onehot[:, oct_par, first + s, j, :],
                                                    e[:, s, j * D:(j + 1) * D], start=(j == 0), stop=(j == PER - 1))
                    last.then_inc(seg_done, 1)

                def put(q, par_q, rows=P, free=True):
                    pe.wait_ge(part_copied, q + 1)
                    pe.wait_ge(place_ready, q + 1)
                    if free:
                        pe.wait_ge(added, q - 1)
                    nc.tensor.matmul(place_ps[par_q % 2][:, 0:P], part[0:rows, par_q % 2, :], place[0:rows, par_q % 2, :],
                                     start=True, stop=True).then_inc(placed, 1)

                def transpose_h(g):
                    pe.wait_ge(h_ready, g + 1)
                    for j in range(PER):
                        last = nc.tensor.transpose(ht_ps[:, j * P:(j + 1) * P], h[:, j, :], ident[:, :])
                    last.then_inc(h_transposed, 1)

                def layer1(g, n0, sums=None):
                    pe.wait_ge(ht_ready, g + 1)
                    if sums is not None:
                        pe.wait_ge(added, sums)
                    nc.tensor.matmul(hid1_ps[:, 0:CHUNK], w1x[:, :], h_t[:, :], start=True, stop=False)
                    nc.tensor.matmul(hid1_ps[:, 0:CHUNK], w1a[:, :], agg[:, bass.ds(n0, CHUNK)],
                                     start=False, stop=True).then_inc(hid1_done, 1)

                def layer2(g):
                    pe.wait_ge(hid1_ready, g + 1)
                    nc.tensor.matmul(hid2_ps[:, 0:CHUNK], w2s[:, :], hid1[:, :], start=True, stop=True).then_inc(hid2_done, 1)

                def layer3(g):
                    pe.wait_ge(hid2_ready, g + 1)
                    pe.wait_ge(y_evacuated, g)
                    for j in range(PER):
                        last = nc.tensor.matmul(y_ps[:, j * D:(j + 1) * D], hid2[:, j, :], w3s[:, :], start=True, stop=True)
                    last.then_inc(y_done, 1)

                def fast():
                    pe.wait_ge(wts_loaded, 9 * 16)
                    for q in range(AHEAD):
                        seg(q, q, 16, q // 2 + 1)
                        if q >= 1:
                            put(q - 1, q - 1, free=q >= 3)

                    def step(i, par, pairs):
                        for k, work in enumerate((lambda: transpose_h(i), lambda: layer1(i, i * CHUNK, 4 * i + AHEAD - 1),
                                                  lambda: layer2(i), lambda: layer3(i))):
                            turn_q = 4 * par + AHEAD + k
                            q = 4 * i + AHEAD + k
                            seg(q, turn_q, 16 * (pairs + turn_q // RING + 1),
                                2 * i + AHEAD // 2 + k // 2 + 1 if k % 2 == 0 else None)
                            put(q - 1, turn_q - 1)
                            work()

                    step(0, 0, 0)
                    with pe.Fori(0, HALVES // 2) as t:
                        step(2 * t + 1, 1, t)
                        step(2 * t + 2, 0, t + 1)

                    slot = QUADS % RING
                    pe.wait_ge(onehot_ready, QUADS // 2 + 1)
                    pe.wait_ge(edges_loaded[slot], 16 * (QUADS // RING + 1))
                    for j in range(PER):
                        last = nc.tensor.matmul(part_ps[QUADS % 2][0:WIN, 0:D], onehot[:, (QUADS // 2) % 2, 0, j, :],
                                                ring[:, slot, j * D:(j + 1) * D], start=(j == 0), stop=(j == PER - 1))
                    last.then_inc(seg_done, 1)
                    put(QUADS - 1, QUADS - 1)
                    transpose_h(GROUPS - 1)
                    put(QUADS, QUADS, rows=WIN)
                    layer1(GROUPS - 1, (GROUPS - 1) * CHUNK, QUADS - 1)
                    transpose_h(GROUPS)
                    layer2(GROUPS - 1)
                    layer1(GROUPS, LAST0, QUADS + 1)
                    layer3(GROUPS - 1)
                    layer2(GROUPS)
                    layer3(GROUPS)

                def general():
                    pe.wait_ge(wts_loaded, 9 * 16)
                    pe.wait_ge(zeros_ready, 1)
                    pe.wait_ge(rest_loaded, 16)
                    acc = part_ps[0]

                    def triple(lhs, n, par, count, stop=False):
                        pe.wait_ge(dense_ready, count)
                        for c in range(n):
                            rows = lhs(c).shape[0]
                            last = nc.tensor.matmul(acc[:, :], lhs(c), ring[0:rows, 2 + par, c * BANK:(c + 1) * BANK],
                                                    start=False, stop=stop and c == n - 1)
                        last.then_inc(dense_used, 1)
                        return last

                    with pe.Fori(0, WINDOWS) as w:
                        pe.wait_ge(window_free, w + 1)
                        nc.tensor.matmul(acc[:, :], place[:, 0, :], iota[:, :], start=True, stop=False)
                        with pe.Fori(0, BLOCKS // 2) as b:
                            for par in range(2):
                                pe.wait_ge(block_loaded[par], w * (8 * BLOCKS) + b * 16 + 16)
                                for k in range(BLOCK // 3):
                                    triple(lambda c: ring[:, par, (3 * k + c) * D:(3 * k + c + 1) * D], 3, k % 2,
                                           w * TRIPLES + b * (2 * BLOCK // 3) + par * (BLOCK // 3) + k + 1)
                                nc.tensor.matmul(place_ps[0][0:1, 0:1], ident[:, 0:1], ident[:, 0:1],
                                                 start=True, stop=True).then_inc(block_done, 1)
                        triple(lambda c: ring[0:RP, 4, c * D:(c + 1) * D], 3, 0, w * TRIPLES + TRIPLES - 1)
                        triple(lambda c: ring[0:RP, 4, (3 + c) * D:(4 + c) * D], RC - 3, 1, w * TRIPLES + TRIPLES, stop=True)
                        nc.tensor.matmul(place_ps[0][0:1, 0:1], ident[:, 0:1], ident[:, 0:1],
                                         start=True, stop=True).then_inc(window_done, 1)
                    pe.wait_ge(window_free, WINDOWS + 1)

                    def group(g, n0):
                        transpose_h(g)
                        layer1(g, n0)
                        layer2(g)
                        layer3(g)

                    with pe.Fori(0, GROUPS) as g:
                        group(g, g * CHUNK)
                    group(GROUPS, LAST0)

                branch(pe, fast, general)

            @block.scalar
            def _(act):
                for t, a in ((w1x, w1[0:P, :]), (w1a, w1[P:2 * P, :]), (w2s, w2), (w3s, w3),
                             (b1s, b1.rearrange("(p o) -> p o", o=1)), (b2s, b2.rearrange("(p o) -> p o", o=1)),
                             (b3s, b3.rearrange("(o f) -> o f", o=1).to_broadcast([P, D])),
                             (lnws, lnw.rearrange("(o f) -> o f", o=1).to_broadcast([P, D])),
                             (lnbs, lnb.rearrange("(o f) -> o f", o=1).to_broadcast([P, D]))):
                    act.dma_start(t[:, :], a).then_inc(wts_loaded, 16)
                act.wait_ge(least_t_done, 1)
                nc.scalar.activation(least_row[0:1, 0:4 * P], part_ps[0][0:1, :], ACT.Copy)
                nc.scalar.activation(least_row[0:1, 4 * P:NCOL], part_ps[1][0:1, 0:NCOL - 4 * P], ACT.Copy).then_inc(least_row_ready, 1)
                banks = [ht_ps, hid1_ps, hid2_ps]
                for t in range(ROWT):
                    act.wait_ge(local_t_done, t + 1)
                    nc.scalar.activation(local_t[:, :, t * P:(t + 1) * P],
                                         banks[t % 3][:, 0:CHUNK].rearrange("p (j s) -> p j s", j=PER), ACT.Copy
                                         ).then_inc(local_t_ready, 1)

                def copy_part(q, par_q, rows=P):
                    act.wait_ge(seg_done, q + 1)
                    nc.scalar.activation(part[0:rows, par_q % 2, :], part_ps[par_q % 2][0:rows, 0:D], ACT.Copy
                                         ).then_inc(part_copied, 1)

                def x_sqrt(g):
                    act.wait_ge(x_mv_ready, g + 1)
                    nc.scalar.activation(x_std[:, :], x_mv[:, :, 1], ACT.Sqrt, bias=eps[:, 0:1]).then_inc(x_std_ready, 1)

                def normalise(g):
                    act.wait_ge(x_shift_ready, g + 1)
                    for j in range(PER):
                        last = nc.scalar.activation(h[:, j, :], xg(g, j), ACT.Relu, bias=x_shift[:, j:j + 1], scale=x_rstd[:, j:j + 1])
                    last.then_inc(h_ready, 1)

                def copy_ht(g):
                    act.wait_ge(h_transposed, g + 1)
                    nc.scalar.activation(h_t[:, :].rearrange("f (p j) -> f j p", j=PER),
                                         ht_ps[:, 0:CHUNK].rearrange("f (j p) -> f j p", j=PER), ACT.Copy).then_inc(ht_ready, 1)

                def relu1(g):
                    act.wait_ge(hid1_done, g + 1)
                    nc.scalar.activation(hid1[:, :], hid1_ps[:, 0:CHUNK], ACT.Relu, bias=b1s[:, 0:1]).then_inc(hid1_ready, 1)

                def relu2(g):
                    act.wait_ge(hid2_done, g + 1)
                    nc.scalar.activation(hid2[:, :, :], hid2_ps[:, 0:CHUNK].rearrange("f (p j) -> f j p", j=PER), ACT.Relu,
                                         bias=b2s[:, 0:1]).then_inc(hid2_ready, 1)

                def y_sqrt(g):
                    act.wait_ge(y_mv_ready, g + 1)
                    nc.scalar.activation(y_std[:, :], y_mv[:, :, 1], ACT.Sqrt, bias=eps[:, 0:1]).then_inc(y_std_ready, 1)

                def fast():
                    act.wait_ge(wts_loaded, 9 * 16)
                    x_sqrt(0)
                    normalise(0)
                    for q in range(AHEAD):
                        copy_part(q, q)

                    def step(i, first):
                        q = 4 * i + AHEAD
                        copy_part(q, AHEAD)
                        copy_ht(i)
                        copy_part(q + 1, AHEAD + 1)
                        relu1(i)
                        x_sqrt(i + 1)
                        copy_part(q + 2, AHEAD + 2)
                        relu2(i)
                        normalise(i + 1)
                        copy_part(q + 3, AHEAD + 3)
                        if not first:
                            y_sqrt(i - 1)

                    step(0, True)
                    with act.Fori(1, HALVES) as i:
                        step(i, False)
                    g = GROUPS - 1
                    copy_part(QUADS, QUADS, rows=WIN)
                    copy_ht(g)
                    y_sqrt(g - 1)
                    relu1(g)
                    x_sqrt(GROUPS)
                    normalise(GROUPS)
                    copy_ht(GROUPS)
                    relu2(g)
                    relu1(GROUPS)
                    act.wait_ge(y_done, GROUPS)
                    relu2(GROUPS)
                    y_sqrt(g)
                    y_sqrt(GROUPS)

                def general():
                    act.wait_ge(wts_loaded, 9 * 16)

                    def group(g):
                        x_sqrt(g)
                        normalise(g)
                        copy_ht(g)
                        relu1(g)
                        relu2(g)
                        y_sqrt(g)

                    with act.Fori(0, GROUPS) as g:
                        group(g)
                    group(GROUPS)

                branch(act, fast, general)

            @block.gpsimd
            def _(pool):
                kw = dict(allow_small_or_imprecise_dtypes=True)
                nc.gpsimd.iota(iota[:, :], [[1, BANK]], base=0, channel_multiplier=0, **kw)
                nc.gpsimd.iota(pidx[:, :], [[0, 1]], base=0, channel_multiplier=1, **kw)
                nc.gpsimd.iota(turn[:, :], [[P * NODES_PER_CHUNK, ROWT]], base=-SLACK, channel_multiplier=NODES_PER_CHUNK,
                               **kw).then_inc(iotas_ready, 1)
                nc.gpsimd.memset(agg[:, :], 0.0).then_inc(agg_zeroed, 1)

                def rows_of(q, n, made):
                    if made:
                        pool.wait_ge(place_ready, q)
                    nc.gpsimd.tensor_copy(rows_at[:, 0:n], row_at[:, bass.ds(q, n)]).then_inc(rows_ready, 1)

                def placement(q, par_q, k, count, free=True):
                    if k == 0:
                        pool.wait_ge(rows_ready, count)
                    if free:
                        pool.wait_ge(placed, q - 1)
                        pool.sem_inc(pool_went_on, 1)
                    nc.gpsimd.tensor_scalar(place[:, par_q % 2, :], iota[:, 0:P], rows_at[:, k:k + 1], None,
                                            ALU.is_equal).then_inc(place_ready, 1)

                def bias_x(g):
                    pool.wait_ge(h_ready, g + 1)
                    v = xg(g).rearrange("p (j f) -> p j f", j=PER)
                    nc.gpsimd.tensor_tensor(v, v, lnbs[:, :].unsqueeze(1).to_broadcast([P, PER, D]), ALU.add).then_inc(x_biased, 1)

                def fast():
                    pool.wait_ge(wts_loaded, 9 * 16)
                    rows_of(0, AHEAD, False)
                    for q in range(2):
                        placement(q, q, q, 1, free=False)
                    bias_x(0)
                    for q in range(2, AHEAD):
                        placement(q, q, q, 1)

                    def step(i):
                        rows_of(4 * i + AHEAD, 4, True)
                        for k in range(4):
                            placement(4 * i + AHEAD + k, k, k, i + 2)
                        bias_x(i + 1)

                    with pool.Fori(0, HALVES) as i:
                        step(i)
                    rows_of(QUADS, 1, True)
                    placement(QUADS, QUADS, 0, HALVES + 2)
                    bias_x(GROUPS)

                def general():
                    pool.wait_ge(wts_loaded, 9 * 16)
                    with pool.Fori(0, GROUPS + 1) as g:
                        bias_x(g)

                branch(pool, fast, general)

            @block.vector
            def _(dve):
                nc.vector.memset(dst_i[:, ROWT - 1, :], 0).then_inc(dst_padded, 1)
                nc.vector.memset(base_i[:, :], 0)
                nc.vector.memset(eps[:, :], EPS)
                nc.vector.memset(signs[0:1, 0, :], 1.0)
                nc.vector.memset(signs[0:1, 1, :], -1.0)
                nc.vector.memset(excess[:, :], -1.0)
                dve.wait_ge(iotas_ready, 1)
                nc.vector.tensor_scalar(ident[:, :], iota[:, 0:P], pidx[:, 0:1], None, ALU.is_equal).then_inc(ident_ready, 1)
                for s in range(QC):
                    rows = slice(s * WIN, (s + 1) * WIN)
                    nc.vector.tensor_scalar(widx[rows, :], pidx[rows, :], float(s * WIN), None, ALU.subtract)
                dve.wait_ge(dst_loaded, 3 * 16)
                nc.vector.tensor_reduce(least[:, :], dst_i[:, :, :], AX.X, ALU.min).then_inc(least_ready, 1)
                dve.wait_ge(least_ready, 1)
                nc.vector.tensor_tensor(local3, dst_i[:, :, :], least[:, :].unsqueeze(2).to_broadcast([P, ROWT, CHUNK]),
                                        ALU.subtract).then_inc(local_ready, 1)
                dve.wait_ge(local_ready, 1)
                nc.vector.tensor_reduce(span[:, :], local3, AX.X, ALU.max)
                nc.vector.tensor_tensor(turn[:, :], turn[:, :], least[:, :], ALU.subtract).then_inc(span_ready, 1)
                dve.wait_ge(least_row_ready, 1)
                nc.vector.tensor_copy(base_i[0:1, 3:3 + QUADS + 1], least_row[0:1, 0:4 * QUADS + 1:QC]).then_inc(base_ready, 1)
                dve.wait_ge(row_at_done, 1)
                nc.vector.tensor_scalar(row_at[:, :], place_ps[0][:, 0:QUADS + 1], widx[:, 0:1], None, ALU.add).then_inc(row_at_ready, 1)
                dve.wait_ge(span_ready, 1)
                dve.wait_ge(row_at_ready, 1)
                nc.vector.tensor_reduce(excess[:, 0:1], span[:, :], AX.X, ALU.max)
                nc.vector.tensor_reduce(excess[:, 1:2], row_at[:, 0:QUADS], AX.X, ALU.max)
                nc.vector.tensor_reduce(excess[:, 2:3], row_at[:, 0:QUADS], AX.X, ALU.min)
                nc.vector.tensor_reduce(excess[:, 3:4], turn[:, 0:ROWT - 1], AX.X, ALU.max)
                nc.vector.tensor_copy(excess[0:LROW + 1, 4:5], turn[0:LROW + 1, ROWT - 1:ROWT]).then_inc(span_ready, 1)
                dve.wait_ge(span_ready, 2)
                nc.vector.tensor_scalar(excess[:, 0:1], excess[:, 0:1], float(WIN - 1), None, ALU.subtract)
                nc.vector.tensor_scalar(excess[:, 1:2], excess[:, 1:2], float(P - 1), None, ALU.subtract)
                nc.vector.tensor_scalar(excess[:, 2:3], excess[:, 2:3], -1.0, None, ALU.mult).then_inc(span_ready, 1)
                dve.wait_ge(span_ready, 3)
                nc.vector.tensor_reduce(excess1[:, 0:1], excess[:, :], AX.X, ALU.max).then_inc(excess_ready, 1)
                dve.wait_ge(local_t_ready, ROWT)
                whole = DONE // PER
                nc.vector.memset(local_t[0:whole, DONE % PER:PER, CHUNKS:CHUNKS + 1], -1.0)
                nc.vector.memset(local_t[0:whole + 1, 0:DONE % PER, CHUNKS:CHUNKS + 1], -1.0).then_inc(tail_masked, 1)
                dve.wait_ge(excess_t_done, 1)
                nc.vector.tensor_reduce(worst[:, :], place_ps[1][0:1, 0:P], AX.X, ALU.max).then_inc(worst_ready, 1)
                dve.wait_ge(worst_ready, 1)
                nc.vector.tensor_scalar(flag_i[:, :], worst[:, :], 0.0, None, ALU.is_le).then_inc(flag_ready, 1)

                def make_onehot(m, par, free=True):
                    if free:
                        dve.wait_ge(seg_done, 2 * m - 2)
                    nc.vector.tensor_tensor(
                        onehot[:, par % 2, :, :, :],
                        iota[:, 0:WIN].unsqueeze(1).unsqueeze(1).to_broadcast([P, OCT, PER, WIN]),
                        local_t[:, :, bass.ds(m * OCT, OCT)].rearrange("p j s -> p s j").unsqueeze(3).to_broadcast([P, OCT, PER, WIN]),
                        ALU.is_equal).then_inc(onehot_ready, 1)

                def bases(q0, n):
                    _, values = nc.values_load_multi_w_load_instructions(
                        base_i[0:1, bass.ds(q0 + 3, n)], engines=[mybir.EngineType.DVE], min_val=0, max_val=AGG - P,
                        skip_runtime_bounds_check_because="the least of dst, which names a node")
                    return values

                def add(q, par_q, base):
                    dve.wait_ge(placed, q + 1)
                    if not (isinstance(q, int) and q == 0):
                        dve.wait_ge(added, q)
                    v = agg[:, bass.ds(base, P)]
                    nc.vector.tensor_tensor(v, place_ps[par_q % 2][:, 0:P], v, ALU.add).then_inc(added, 1)

                def stats_x(g, par, pairs):
                    dve.wait_ge(x_loaded[par], 16 * pairs + 16)
                    for j in range(PER):
                        last = nc.vector.bn_stats(x_stats[:, j, :], xg(g, j))
                    last.then_inc(x_stats_done, 1)

                def mean_x(g):
                    dve.wait_ge(x_stats_done, g + 1)
                    dve.sem_inc(dve_went_on, 1)
                    for j in range(PER):
                        last = nc.vector.bn_aggr(x_mv[:, j, :], x_stats[:, j, :])
                    last.then_inc(x_mv_ready, 1)

                def scale_x(g):
                    dve.wait_ge(x_std_ready, g + 1)
                    nc.vector.reciprocal(x_rstd[:, :], x_std[:, :]).then_inc(x_rstd_done, 1)

                def shift_x(g):
                    dve.wait_ge(x_rstd_done, g + 1)
                    nc.vector.scalar_tensor_tensor(x_shift[:, :], x_mv[:, :, 0], -1.0, x_rstd[:, :], ALU.mult, ALU.mult
                                                   ).then_inc(x_shift_ready, 1)

                def take_y(g):
                    dve.wait_ge(y_done, g + 1)
                    nc.vector.tensor_tensor(y[:, :, :], y_ps[:, 0:CHUNK].rearrange("p (j f) -> p j f", j=PER),
                                            b3s[:, :].unsqueeze(1).to_broadcast([P, PER, D]), ALU.add).then_inc(y_evacuated, 1)

                def stats_y(g):
                    dve.wait_ge(y_evacuated, g + 1)
                    for j in range(PER):
                        last = nc.vector.bn_stats(y_stats[:, j, :], y[:, j, :])
                    last.then_inc(y_stats_done, 1)

                def mean_y(g):
                    dve.wait_ge(y_stats_done, g + 1)
                    dve.sem_inc(dve_went_on, 1)
                    for j in range(PER):
                        last = nc.vector.bn_aggr(y_mv[:, j, :], y_stats[:, j, :])
                    last.then_inc(y_mv_ready, 1)

                def center_y(g):
                    dve.wait_ge(y_mv_ready, g + 1)
                    for j in range(PER):
                        last = nc.vector.scalar_tensor_tensor(z[:, j, :], y[:, j, :], y_mv[:, j, 0:1], lnws[:, :],
                                                              ALU.subtract, ALU.mult)
                    last.then_inc(y_centered, 1)

                def scale_y(g):
                    dve.wait_ge(y_std_ready, g + 1)
                    nc.vector.reciprocal(y_rstd[:, :], y_std[:, :]).then_inc(y_rstd_done, 1)

                def output(g):
                    dve.wait_ge(y_rstd_done, g + 1)
                    dve.wait_ge(y_centered, g + 1)
                    dve.wait_ge(x_biased, g + 1)
                    for j in range(PER):
                        last = nc.vector.scalar_tensor_tensor(xg(g, j), z[:, j, :], y_rstd[:, j:j + 1], xg(g, j),
                                                              ALU.mult, ALU.add)
                    last.then_inc(out_ready, 1)

                def finish(g):
                    take_y(g)
                    stats_y(g)
                    mean_y(g)
                    center_y(g)
                    scale_y(g)
                    output(g)

                def fast():
                    dve.wait_ge(tail_masked, 1)
                    dve.wait_ge(wts_loaded, 9 * 16)
                    make_onehot(0, 0, free=False)
                    make_onehot(1, 1, free=False)
                    stats_x(0, 0, 0)
                    mean_x(0)
                    scale_x(0)
                    shift_x(0)
                    dve.wait_ge(base_ready, 1)
                    dve.wait_ge(agg_zeroed, 1)
                    base = bases(0, AHEAD - 1)
                    add(0, 0, base[0])
                    make_onehot(2, 2)
                    add(1, 1, base[1])
                    add(2, 2, base[2])
                    make_onehot(3, 3)
                    add(3, 3, base[3])
                    add(4, 4, base[4])

                    def step(i, par, pairs, first=False):
                        make_onehot(2 * i + 4, 0)
                        base = bases(4 * i + AHEAD - 1, 4)
                        q = 4 * i + AHEAD - 1
                        add(q, 1, base[0])
                        stats_x(i + 1, 1 - par, pairs + par)
                        if not first:
                            take_y(i - 1)
                        add(q + 1, 0, base[1])
                        mean_x(i + 1)
                        if not first:
                            stats_y(i - 1)
                        scale_x(i + 1)
                        shift_x(i + 1)
                        if not first:
                            mean_y(i - 1)
                        add(q + 2, 1, base[2])
                        if not first:
                            center_y(i - 1)
                        make_onehot(2 * i + 5, 1)
                        add(q + 3, 0, base[3])
                        if not first:
                            scale_y(i - 1)
                            output(i - 1)

                    step(0, 0, 0, first=True)
                    with dve.Fori(0, HALVES // 2) as t:
                        step(2 * t + 1, 1, t)
                        step(2 * t + 2, 0, t + 1)
                    base = bases(QUADS - 1, 2)
                    add(QUADS - 1, 1, base[0])
                    stats_x(GROUPS, GROUPS % 2, GROUPS // 2)
                    take_y(GROUPS - 2)
                    add(QUADS, 0, base[1])
                    mean_x(GROUPS)
                    stats_y(GROUPS - 2)
                    mean_y(GROUPS - 2)
                    center_y(GROUPS - 2)
                    scale_y(GROUPS - 2)
                    output(GROUPS - 2)
                    scale_x(GROUPS)
                    shift_x(GROUPS)
                    finish(GROUPS - 1)
                    finish(GROUPS)

                def general():
                    d2 = dst_i[:, :, :].rearrange("p t k -> p (t k)")
                    cols = BLOCKS * BLOCK + RC
                    dve.wait_ge(tail_masked, 1)
                    dve.wait_ge(agg_zeroed, 1)
                    dve.wait_ge(wts_loaded, 9 * 16)
                    for k in range(RING):
                        dve.wait_ge(edges_loaded[k], 16)
                    nc.vector.memset(place[:, 0, :], 0.0).then_inc(zeros_ready, 1)
                    nc.vector.memset(local[RP:P, BLOCKS * BLOCK:BLOCKS * BLOCK + RC], -1.0)
                    dve.wait_ge(dst2_loaded, 32)
                    nc.vector.tensor_copy(local[:, 0:BLOCKS * BLOCK], d2[:, 0:BLOCKS * BLOCK])
                    nc.vector.tensor_copy(local[0:RP, BLOCKS * BLOCK:cols], d2[0:RP, BLOCKS * BLOCK:cols]).then_inc(dst2_ready, 1)
                    dve.sem_inc(block_done, 2)
                    dve.sem_inc(dense_used, 2)
                    dve.sem_inc(window_free, 1)

                    def dense(col, n, par, count, rows=P):
                        dve.wait_ge(dense_used, count)
                        for c in range(n):
                            last = nc.vector.tensor_scalar(ring[0:rows, 2 + par, c * BANK:(c + 1) * BANK], iota[0:rows, :],
                                                           local[0:rows, bass.ds(col + c, 1)], None, ALU.is_equal)
                        last.then_inc(dense_ready, 1)

                    with dve.Fori(0, WINDOWS) as w:
                        dve.wait_ge(dst2_ready, w + 1)
                        dve.sem_inc(dve_went_on, 1)
                        with dve.Fori(0, BLOCKS) as b:
                            for k in range(BLOCK // 3):
                                dense(b * BLOCK + 3 * k, 3, k % 2, w * TRIPLES + b * (BLOCK // 3) + k + 1)
                        dense(BLOCKS * BLOCK, 3, 0, w * TRIPLES + TRIPLES - 1, RP)
                        dense(BLOCKS * BLOCK + 3, RC - 3, 1, w * TRIPLES + TRIPLES, RP)
                        dve.wait_ge(dense_ready, w * TRIPLES + TRIPLES)
                        nc.vector.tensor_scalar(local[:, 0:cols], local[:, 0:cols], float(BANK), None, ALU.subtract).then_inc(dst2_ready, 1)
                        dve.wait_ge(window_done, w + 1)
                        nc.vector.tensor_copy(agg[:, bass.ds(w * BANK, BANK)], part_ps[0][:, :]).then_inc(window_free, 1)

                    def group(g, par, pairs):
                        stats_x(g, par, pairs)
                        mean_x(g)
                        scale_x(g)
                        shift_x(g)
                        finish(g)

                    with dve.Fori(0, GROUPS // 2) as t:
                        group(2 * t, 0, t)
                        group(2 * t + 1, 1, t)
                    group(GROUPS, GROUPS % 2, GROUPS // 2)

                branch(dve, fast, general)


_INS = ["x", "dst", "edge_attr_128", "L0_gnn_W1", "L0_gnn_b1", "L0_gnn_W2", "L0_gnn_b2", "L0_gnn_W3", "L0_gnn_b3",
        "L0_gnn_ln_w", "L0_gnn_ln_b"]


def kernel(**inputs):
    import concourse.bacc as bacc
    from concourse.bass_utils import run_bass_kernel_spmd

    nc = bacc.Bacc("TRN2", target_bir_lowering=False, num_devices=1)
    arrays, args = {}, []
    for name in _INS:
        a = np.ascontiguousarray(inputs[name])
        arrays[f"in_{name}"] = a
        args.append(nc.dram_tensor(f"in_{name}", a.shape, mybir.dt.from_np(a.dtype), kind="ExternalInput").ap())
    args.append(nc.dram_tensor("out_x", (NODES, D), F32, kind="ExternalOutput").ap())
    gnn_kernel(nc, *args)
    r = run_bass_kernel_spmd(nc, [arrays], core_ids=[0])
    return r.results[0]["out_x"]
```

```python
from contextlib import ExitStack

import numpy as np

import concourse.bass as bass
from concourse import mybir

F32 = mybir.dt.float32
I32 = mybir.dt.int32
ALU = mybir.AluOpType
ACT = mybir.ActivationFunctionType
AX = mybir.AxisListType

P = 128
NODES, EDGES, D = 12500, 200000, 128
EPS = 1e-5

PER = 3
CHUNK = P * PER
WIN = 32
QC = P // WIN
QUAD = QC * CHUNK
QUADS = EDGES // QUAD
CHUNKS = QUADS * QC
TAIL0 = EDGES - CHUNK
DONE = CHUNKS * CHUNK - TAIL0
OCT = 2 * QC
GROUPS = NODES // CHUNK
LAST = GROUPS
LAST0 = GROUPS * CHUNK
LAST_PER = 2
LAST_N = NODES - LAST0
LAST_P = LAST_N // LAST_PER
LAST_CUT = LAST_P // 16 * 16
LAST_PARTS = ((0, LAST_CUT), (LAST_CUT, LAST_P))
ROWT = -(-(CHUNKS + 1) // P)
LROW = CHUNKS - (ROWT - 1) * P
NCOL = ROWT * P
RING = 8
SLACK = 96
NODES_PER_CHUNK = 24
BANK = 512
WINDOWS = -(-NODES // BANK)
AGG = WINDOWS * BANK
BLOCK = 12
BLOCKS = EDGES // (P * BLOCK)
REST = EDGES - BLOCKS * P * BLOCK
RP = 64
RC = REST // RP
TRIPLES = BLOCKS * BLOCK // 3 + 2
XAHEAD = 3
AHEAD = 6
STORED_EARLY = 8
STEPS = GROUPS - 1


def gnn_kernel(nc, x, dst, edges, w1, b1, w2, b2, w3, b3, lnw, lnb, out):
    assert GROUPS == 32 and QUADS == 4 * STEPS + AHEAD and LAST_P * LAST_PER == LAST_N and RC * RP == REST
    with ExitStack() as ctx:
        def sb(name, shape, dt=F32):
            return ctx.enter_context(nc.sbuf_tensor(name, shape, dt))

        def sem(name):
            return ctx.enter_context(nc.semaphore(name))

        ring = sb("ring", [P, RING, QC * PER * D])
        agg = sb("agg", [P, AGG])
        xs = sb("xs", [P, GROUPS * CHUNK + LAST_PER * D])
        dst_i = sb("dst_i", [P, ROWT, CHUNK], I32)
        local = sb("local", [P, ROWT * CHUNK])
        local3 = local[:, :].rearrange("p (t k) -> p t k", t=ROWT)
        local_t = sb("local_t", [P, PER, NCOL])
        onehot = sb("onehot", [P, 2, OCT, PER, WIN])
        part = sb("part", [P, 2, D])
        place = sb("place", [P, 2, P])
        iota = sb("iota", [P, BANK])
        ident = sb("ident", [P, P])
        pidx = sb("pidx", [P, 1])
        widx = sb("widx", [P, 1])
        least = sb("least", [P, ROWT])
        turn = sb("turn", [P, ROWT])
        span = sb("span", [P, ROWT])
        least_row = sb("least_row", [1, NCOL])
        base_i = sb("base_i", [1, 3 + QUADS + 1 + 2], I32)
        row_at = sb("row_at", [P, QUADS + 1])
        rows_at = sb("rows_at", [P, AHEAD])
        excess = sb("excess", [P, 5])
        excess1 = sb("excess1", [P, 1])
        worst = sb("worst", [1, 1])
        flag_i = sb("flag_i", [1, 1], I32)
        signs = sb("signs", [1, 2, P])
        eps = sb("eps", [P, 1])
        root = sb("root", [P, 1])
        w1x = sb("w1x", [P, P])
        w1a = sb("w1a", [P, P])
        w2s = sb("w2s", [P, P])
        w3s = sb("w3s", [P, P])
        b1s = sb("b1s", [P, 1])
        b2s = sb("b2s", [P, 1])
        b3s = sb("b3s", [P, D])
        lnws = sb("lnws", [P, D])
        lnbs = sb("lnbs", [P, D])
        x_stats = sb("x_stats", [P, PER, 6])
        x_mv = sb("x_mv", [P, PER, 2])
        x_std = sb("x_std", [P, PER])
        x_rstd = sb("x_rstd", [P, PER])
        x_shift = sb("x_shift", [P, PER])
        h = sb("h", [P, PER, D])
        h_t = sb("h_t", [P, CHUNK])
        h_last_t = sb("h_last_t", [P, LAST_N])
        hid1 = sb("hid1", [P, CHUNK])
        hid2 = sb("hid2", [P, PER, P])
        y = sb("y", [P, PER, D])
        z = sb("z", [P, PER, D])
        y_stats = sb("y_stats", [P, PER, 6])
        y_mv = sb("y_mv", [P, PER, 2])
        y_std = sb("y_std", [P, PER])
        y_rstd = sb("y_rstd", [P, PER])
        y_last_rstd = sb("y_last_rstd", [P, LAST_PER])

        def bank(name):
            return ctx.enter_context(nc.psum_tensor(name, [P, BANK], F32))

        part_ps = [bank("part_ps0"), bank("part_ps1")]
        place_ps = [bank("place_ps0"), bank("place_ps1")]
        ht_ps, hid1_ps, hid2_ps, y_ps = bank("ht_ps"), bank("hid1_ps"), bank("hid2_ps"), bank("y_ps")
        y_last_ps = part_ps[1]

        dst_padded = sem("dst_padded")
        dst_loaded = sem("dst_loaded")
        x_loaded = [sem("x_loaded_even"), sem("x_loaded_odd")]
        last_x_loaded = sem("last_x_loaded")
        wts_loaded = sem("wts_loaded")
        iotas_ready = sem("iotas_ready")
        eps_ready = sem("eps_ready")
        ident_ready = sem("ident_ready")
        agg_zeroed = sem("agg_zeroed")
        least_ready = sem("least_ready")
        local_ready = sem("local_ready")
        span_ready = sem("span_ready")
        least_t_done = sem("least_t_done")
        least_row_ready = sem("least_row_ready")
        local_t_done = sem("local_t_done")
        local_t_ready = sem("local_t_ready")
        tail_masked = sem("tail_masked")
        base_ready = sem("base_ready")
        row_at_done = sem("row_at_done")
        row_at_ready = sem("row_at_ready")
        excess_ready = sem("excess_ready")
        excess_t_done = sem("excess_t_done")
        worst_ready = sem("worst_ready")
        flag_ready = sem("flag_ready")
        edges_loaded = [sem(f"edges_loaded{k}") for k in range(RING)]
        onehot_ready = sem("onehot_ready")
        seg_done = sem("seg_done")
        part_copied = sem("part_copied")
        rows_ready = sem("rows_ready")
        place_ready = sem("place_ready")
        placed = sem("placed")
        added = sem("added")
        dve_went_on = sem("dve_went_on")
        pool_went_on = sem("pool_went_on")
        dst2_loaded = sem("dst2_loaded")
        dst2_ready = sem("dst2_ready")
        block_loaded = [sem("block_loaded0"), sem("block_loaded1")]
        rest_loaded = sem("rest_loaded")
        block_done = sem("block_done")
        dense_ready = sem("dense_ready")
        dense_used = sem("dense_used")
        zeros_ready = sem("zeros_ready")
        window_done = sem("window_done")
        window_free = sem("window_free")
        x_stats_done = sem("x_stats_done")
        x_mv_ready = sem("x_mv_ready")
        x_std_ready = sem("x_std_ready")
        x_rstd_done = sem("x_rstd_done")
        x_shift_ready = sem("x_shift_ready")
        h_ready = sem("h_ready")
        h_transposed = sem("h_transposed")
        ht_ready = sem("ht_ready")
        x_biased = sem("x_biased")
        hid1_done = sem("hid1_done")
        hid1_ready = sem("hid1_ready")
        hid2_done = sem("hid2_done")
        hid2_ready = sem("hid2_ready")
        y_done = sem("y_done")
        y_evacuated = sem("y_evacuated")
        y_stats_done = sem("y_stats_done")
        y_mv_ready = sem("y_mv_ready")
        y_std_ready = sem("y_std_ready")
        y_rstd_done = sem("y_rstd_done")
        y_centered = sem("y_centered")
        out_ready = sem("out_ready")
        z_scaled = sem("z_scaled")
        full_out_ready = sem("full_out_ready")
        stored = sem("stored")

        def quad_of_edges(q):
            return edges[bass.ds(q * QUAD, QUAD), :].rearrange("(s p j) f -> p s (j f)", p=P, j=PER)

        def ring_slot(k):
            return ring[:, k, :].rearrange("p (s e) -> p s e", s=QC)

        def shape(g):
            return (LAST_P, LAST_PER) if isinstance(g, int) and g == LAST else (P, PER)

        def nth(g):
            return 1 if isinstance(g, int) and g == LAST else g + 2

        def group_rows(t, g):
            rows, per = shape(g)
            return t[bass.ds(g * CHUNK, rows * per), :].rearrange("(p j) f -> p (j f)", j=per)

        def last_rows(t, p0, p1):
            return t[LAST0 + p0 * LAST_PER:LAST0 + p1 * LAST_PER, :].rearrange("(p j) f -> p (j f)", j=LAST_PER)

        def xg(g, j=None):
            rows, per = shape(g)
            if j is None:
                return xs[0:rows, bass.ds(g * CHUNK, per * D)]
            return xs[0:rows, bass.ds(g * CHUNK + j * D, D)]

        def branch(eng, fast, general):
            eng.wait_ge(flag_ready, 1)
            fits = eng.value_load(flag_i[0:1, 0:1])
            with eng.If(fits != 0):
                fast()
            with eng.Else():
                general()

        with nc.Block() as block:

            @block.sync
            def _(sp):
                full = (ROWT - 1) * P
                sp.dma_start(dst_i[:, 0:ROWT - 1, :],
                             dst[0:full * CHUNK].rearrange("(t p k) -> p t k", p=P, k=CHUNK)).then_inc(dst_loaded, 16)
                sp.wait_ge(dst_padded, 1)
                sp.dma_start(dst_i[0:LROW, ROWT - 1, :],
                             dst[full * CHUNK:CHUNKS * CHUNK].rearrange("(p k) -> p k", k=CHUNK)).then_inc(dst_loaded, 16)
                sp.dma_start(dst_i[LROW:LROW + 1, ROWT - 1, :],
                             dst[TAIL0:EDGES].rearrange("(p k) -> p k", k=CHUNK)).then_inc(dst_loaded, 16)

                def load_x(g, par, before):
                    if not (isinstance(before, int) and before == 0):
                        sp.wait_ge(x_loaded[par], 16 * before)
                    sp.dma_start(xg(g), group_rows(x, g)).then_inc(x_loaded[par], 16)

                sp.dma_start(ring_slot(0), quad_of_edges(0)).then_inc(edges_loaded[0], 16)
                for p0, p1 in LAST_PARTS:
                    sp.dma_start(xg(LAST)[p0:p1, :], last_rows(x, p0, p1)).then_inc(last_x_loaded, 16)
                load_x(0, 0, 0)
                load_x(1, 1, 0)
                for q in range(1, RING):
                    sp.dma_start(ring_slot(q), quad_of_edges(q)).then_inc(edges_loaded[q], 16)
                for g in range(2, XAHEAD):
                    load_x(g, g % 2, g // 2)

                def store(g):
                    sp.wait_ge(out_ready, g + 1)
                    sp.dma_start(group_rows(out, g), xg(g)).then_inc(stored, 16)

                def store_last(count):
                    sp.wait_ge(out_ready, count)
                    for p0, p1 in LAST_PARTS:
                        sp.dma_start(last_rows(out, p0, p1), xg(LAST)[p0:p1, :]).then_inc(stored, 16)

                def store_two(g):
                    sp.wait_ge(out_ready, g + 2)
                    sp.dma_start(out[bass.ds(g * CHUNK, 2 * CHUNK), :].rearrange("(g p j) f -> p g (j f)", p=P, j=PER),
                                 xs[:, bass.ds(g * CHUNK, 2 * CHUNK)].rearrange("p (g e) -> p g e", g=2)).then_inc(stored, 16)

                def reload(q, slot):
                    sp.wait_ge(seg_done, q - RING + 1)
                    sp.dma_start(ring_slot(slot), quad_of_edges(q)).then_inc(edges_loaded[slot], 16)

                def fast():
                    for q in range(RING, RING + AHEAD):
                        reload(q, q % RING)

                    def step(i, par, pairs):
                        load_x(i + XAHEAD, (par + XAHEAD) % 2, pairs + (par + XAHEAD) // 2)
                        for k in range(4):
                            reload(4 * i + RING + AHEAD + k, (4 * par + AHEAD + k) % RING)

                    step(0, 0, 0)
                    with sp.Fori(0, STORED_EARLY // 2) as t:
                        step(2 * t + 1, 1, t)
                        step(2 * t + 2, 0, t + 1)
                        store_two(2 * t)
                    with sp.Fori(STORED_EARLY // 2, (STEPS - 3) // 2) as t:
                        step(2 * t + 1, 1, t)
                        step(2 * t + 2, 0, t + 1)
                    sp.wait_ge(seg_done, QUADS - RING + 1)
                    tail = QUADS % RING
                    sp.dma_start(ring[:, tail, 0:PER * D],
                                 edges[TAIL0:EDGES, :].rearrange("(p j) f -> p (j f)", j=PER)).then_inc(edges_loaded[tail], 16)
                    for g in range(STORED_EARLY, GROUPS - 2, 2):
                        store_two(g)
                    store(GROUPS - 2)
                    store_last(GROUPS)
                    sp.wait_ge(stored, 16 * ((GROUPS - 2) // 2 + 2 + len(LAST_PARTS)))

                def general():
                    d2 = dst_i[:, :, :].rearrange("p t k -> p (t k)")
                    sp.dma_start(d2[:, 0:BLOCKS * BLOCK].rearrange("p (b c) -> p b c", c=BLOCK),
                                 dst[0:BLOCKS * P * BLOCK].rearrange("(b p c) -> p b c", p=P, c=BLOCK)
                                 ).then_inc(dst2_loaded, 16)
                    sp.dma_start(d2[0:RP, BLOCKS * BLOCK:BLOCKS * BLOCK + RC],
                                 dst[EDGES - REST:EDGES].rearrange("(p c) -> p c", c=RC)).then_inc(dst2_loaded, 16)
                    for k in range(RING):
                        sp.wait_ge(edges_loaded[k], 16)
                    sp.dma_start(ring[0:RP, 4, 0:RC * D],
                                 edges[EDGES - REST:EDGES, :].rearrange("(p c) f -> p (c f)", c=RC)).then_inc(rest_loaded, 16)
                    with sp.Fori(0, WINDOWS) as w:
                        with sp.Fori(0, BLOCKS // 2) as b:
                            for par in range(2):
                                sp.wait_ge(block_done, w * BLOCKS + 2 * b + par + 1)
                                sp.dma_start(ring[:, par, :],
                                             edges[bass.ds((2 * b + par) * P * BLOCK, P * BLOCK), :]
                                             .rearrange("(p c) f -> p (c f)", c=BLOCK)).then_inc(block_loaded[par], 16)
                    load_x(XAHEAD, XAHEAD % 2, XAHEAD // 2)
                    with sp.Fori(2, GROUPS // 2) as t:
                        load_x(2 * t, 0, t)
                        load_x(2 * t + 1, 1, t)
                    with sp.Fori(0, GROUPS) as g:
                        store(g)
                    store_last(GROUPS + 1)
                    sp.wait_ge(stored, 16 * (GROUPS + len(LAST_PARTS)))

                branch(sp, fast, general)

            @block.tensor
            def _(pe):
                pe.wait_ge(least_ready, 1)
                pe.wait_ge(ident_ready, 1)
                for t in range(ROWT):
                    row = part_ps[t // 4][0:1, (t % 4) * P:(t % 4 + 1) * P]
                    last = nc.tensor.matmul(row, least[:, t:t + 1], ident[:, :], start=True, stop=True)
                last.then_inc(least_t_done, 1)
                pe.wait_ge(local_ready, 1)
                banks = [ht_ps, hid1_ps, hid2_ps]
                for t in range(ROWT):
                    if t >= len(banks):
                        pe.wait_ge(local_t_ready, t - len(banks) + 1)
                    for j in range(PER):
                        last = nc.tensor.transpose(banks[t % 3][:, j * P:(j + 1) * P], local3[:, t, j::PER], ident[:, :])
                    last.then_inc(local_t_done, 1)
                pe.wait_ge(least_row_ready, 1)
                for s in range(QC):
                    o = place_ps[0][s * WIN:(s + 1) * WIN, 0:QUADS + 1]
                    nc.tensor.matmul(o, signs[0:1, 0, 0:WIN], least_row[0:1, s:s + 4 * QUADS + 1:QC], start=True, stop=False)
                    last = nc.tensor.matmul(o, signs[0:1, 1, 0:WIN], least_row[0:1, 0:4 * QUADS + 1:QC], start=False, stop=True)
                last.then_inc(row_at_done, 1)
                pe.wait_ge(excess_ready, 1)
                nc.tensor.matmul(place_ps[1][0:1, 0:P], excess1[:, 0:1], ident[:, :], start=True, stop=True).then_inc(excess_t_done, 1)

                def seg(q, par_q, load_count, oct_ready=None):
                    slot = par_q % RING
                    pe.wait_ge(edges_loaded[slot], load_count)
                    if oct_ready is not None:
                        pe.wait_ge(onehot_ready, oct_ready)
                    e = ring_slot(slot)
                    oct_par, first = (par_q // 2) % 2, (par_q % 2) * QC
                    for j in range(PER):
                        for s in range(QC):
                            last = nc.tensor.matmul(part_ps[par_q % 2][s * WIN:(s + 1) * WIN, 0:D],
                                                    onehot[:, oct_par, first + s, j, :],
                                                    e[:, s, j * D:(j + 1) * D], start=(j == 0), stop=(j == PER - 1))
                    last.then_inc(seg_done, 1)

                def put(q, par_q, rows=P, free=True):
                    pe.wait_ge(part_copied, q + 1)
                    pe.wait_ge(place_ready, q + 1)
                    if free:
                        pe.wait_ge(added, q - 1)
                    nc.tensor.matmul(place_ps[par_q % 2][:, 0:P], part[0:rows, par_q % 2, :], place[0:rows, par_q % 2, :],
                                     start=True, stop=True).then_inc(placed, 1)

                def transpose_h(g):
                    rows, per = shape(g)
                    pe.wait_ge(h_ready, nth(g))
                    if rows == P:
                        pe.wait_ge(ht_ready, nth(g) - 1)
                    for j in range(per):
                        last = nc.tensor.transpose(ht_ps[:, j * rows:(j + 1) * rows], h[0:rows, j, :], ident[0:rows, 0:rows])
                    last.then_inc(h_transposed, 1)

                def layer1_x(g):
                    n = shape(g)[0] * shape(g)[1]
                    pe.wait_ge(ht_ready, nth(g))
                    t = h_t if n == CHUNK else h_last_t
                    nc.tensor.matmul(hid1_ps[:, 0:n], w1x[:, :], t[:, :], start=True, stop=False)

                def layer1_sums(g, sums=None):
                    n = shape(g)[0] * shape(g)[1]
                    if sums is not None:
                        pe.wait_ge(added, sums)
                    nc.tensor.matmul(hid1_ps[:, 0:n], w1a[:, :], agg[:, bass.ds(g * CHUNK, n)],
                                     start=False, stop=True).then_inc(hid1_done, 1)

                def layer1(g, sums=None):
                    layer1_x(g)
                    layer1_sums(g, sums)

                def layer2(g):
                    n = shape(g)[0] * shape(g)[1]
                    pe.wait_ge(hid1_ready, g + 1)
                    nc.tensor.matmul(hid2_ps[:, 0:n], w2s[:, :], hid1[:, 0:n], start=True, stop=True).then_inc(hid2_done, 1)

                def layer3(g):
                    pe.wait_ge(hid2_ready, g + 1)
                    pe.wait_ge(y_evacuated, g)
                    for j in range(PER):
                        last = nc.tensor.matmul(y_ps[:, j * D:(j + 1) * D], hid2[:, j, :], w3s[:, :], start=True, stop=True)
                    last.then_inc(y_done, 1)

                def layer3_last_bias():
                    nc.tensor.matmul(y_last_ps[0:LAST_P, 0:LAST_PER * D].rearrange("p (j f) -> p j f", j=LAST_PER),
                                     signs[0:1, 0, 0:LAST_P],
                                     b3s[0:1, :].unsqueeze(1).to_broadcast([1, LAST_PER, D]), start=True, stop=False)

                def layer3_last():
                    pe.wait_ge(hid2_ready, LAST + 1)
                    for j in range(LAST_PER):
                        last = nc.tensor.matmul(y_last_ps[0:LAST_P, j * D:(j + 1) * D], hid2[:, j, 0:LAST_P], w3s[:, :],
                                                start=False, stop=j == LAST_PER - 1)
                    last.then_inc(y_done, 1)

                transpose_h(LAST)

                def fast():
                    pe.wait_ge(wts_loaded, 9 * 16)
                    for q in range(AHEAD):
                        seg(q, q, 16, q // 2 + 1)
                        if q >= 1:
                            put(q - 1, q - 1, free=q >= 3)
                    transpose_h(0)

                    def step(i, par, pairs):
                        for k in range(4):
                            turn_q = 4 * par + AHEAD + k
                            q = 4 * i + AHEAD + k
                            seg(q, turn_q, 16 * (pairs + turn_q // RING + 1),
                                2 * i + AHEAD // 2 + k // 2 + 1 if k % 2 == 0 else None)
                            put(q - 1, turn_q - 1)
                            if k == 0:
                                layer1(i, 4 * i + AHEAD - 1)
                            elif k == 1:
                                layer2(i)
                            elif k == 2:
                                layer3(i)
                            else:
                                transpose_h(i + 1)

                    step(0, 0, 0)
                    with pe.Fori(0, (STEPS - 3) // 2) as t:
                        step(2 * t + 1, 1, t)
                        step(2 * t + 2, 0, t + 1)
                    step(STEPS - 2, 1, (STEPS - 2) // 2)

                    q, g = QUADS - 4, GROUPS - 2

                    def loads_of(quad):
                        return 16 * (quad // RING + 1)

                    layer1_x(g)
                    seg(q, q, loads_of(q), q // 2 + 1)
                    put(q - 1, q - 1)
                    layer1_sums(g, q - 1)
                    put(q, q)
                    transpose_h(g + 1)
                    seg(q + 1, q + 1, loads_of(q + 1))
                    layer2(g)
                    put(q + 1, q + 1)
                    layer1_x(g + 1)
                    seg(q + 2, q + 2, loads_of(q + 2), q // 2 + 2)
                    layer3(g)
                    put(q + 2, q + 2)
                    seg(q + 3, q + 3, loads_of(q + 3))
                    layer1_sums(g + 1, QUADS - 1)
                    put(q + 3, q + 3)
                    slot = QUADS % RING
                    pe.wait_ge(onehot_ready, QUADS // 2 + 1)
                    pe.wait_ge(edges_loaded[slot], loads_of(QUADS))
                    for j in range(PER):
                        last = nc.tensor.matmul(part_ps[QUADS % 2][0:WIN, 0:D], onehot[:, (QUADS // 2) % 2, 0, j, :],
                                                ring[:, slot, j * D:(j + 1) * D], start=(j == 0), stop=(j == PER - 1))
                    last.then_inc(seg_done, 1)
                    layer2(g + 1)
                    layer1_x(LAST)
                    put(QUADS, QUADS, rows=WIN)
                    layer3_last_bias()
                    layer3(g + 1)
                    layer1_sums(LAST, QUADS + 1)
                    layer2(LAST)
                    layer3_last()

                def general():
                    pe.wait_ge(wts_loaded, 9 * 16)
                    pe.wait_ge(zeros_ready, 1)
                    pe.wait_ge(rest_loaded, 16)
                    acc = part_ps[0]

                    def triple(lhs, n, par, count, stop=False):
                        pe.wait_ge(dense_ready, count)
                        for c in range(n):
                            rows = lhs(c).shape[0]
                            last = nc.tensor.matmul(acc[:, :], lhs(c), ring[0:rows, 2 + par, c * BANK:(c + 1) * BANK],
                                                    start=False, stop=stop and c == n - 1)
                        last.then_inc(dense_used, 1)
                        return last

                    with pe.Fori(0, WINDOWS) as w:
                        pe.wait_ge(window_free, w + 1)
                        nc.tensor.matmul(acc[:, :], place[:, 0, :], iota[:, :], start=True, stop=False)
                        with pe.Fori(0, BLOCKS // 2) as b:
                            for par in range(2):
                                pe.wait_ge(block_loaded[par], w * (8 * BLOCKS) + b * 16 + 16)
                                for k in range(BLOCK // 3):
                                    triple(lambda c: ring[:, par, (3 * k + c) * D:(3 * k + c + 1) * D], 3, k % 2,
                                           w * TRIPLES + b * (2 * BLOCK // 3) + par * (BLOCK // 3) + k + 1)
                                nc.tensor.matmul(place_ps[0][0:1, 0:1], ident[:, 0:1], ident[:, 0:1],
                                                 start=True, stop=True).then_inc(block_done, 1)
                        triple(lambda c: ring[0:RP, 4, c * D:(c + 1) * D], 3, 0, w * TRIPLES + TRIPLES - 1)
                        triple(lambda c: ring[0:RP, 4, (3 + c) * D:(4 + c) * D], RC - 3, 1, w * TRIPLES + TRIPLES, stop=True)
                        nc.tensor.matmul(place_ps[0][0:1, 0:1], ident[:, 0:1], ident[:, 0:1],
                                         start=True, stop=True).then_inc(window_done, 1)
                    pe.wait_ge(window_free, WINDOWS + 1)

                    with pe.Fori(0, GROUPS) as g:
                        transpose_h(g)
                        layer1(g)
                        layer2(g)
                        layer3(g)
                    layer1(LAST)
                    layer2(LAST)
                    layer3_last_bias()
                    layer3_last()

                branch(pe, fast, general)

            @block.scalar
            def _(act):
                for t, a in ((w1x, w1[0:P, :]), (w1a, w1[P:2 * P, :]), (w2s, w2), (w3s, w3),
                             (b1s, b1.rearrange("(p o) -> p o", o=1)), (b2s, b2.rearrange("(p o) -> p o", o=1)),
                             (b3s, b3.rearrange("(o f) -> o f", o=1).to_broadcast([P, D])),
                             (lnws, lnw.rearrange("(o f) -> o f", o=1).to_broadcast([P, D])),
                             (lnbs, lnb.rearrange("(o f) -> o f", o=1).to_broadcast([P, D]))):
                    act.dma_start(t[:, :], a).then_inc(wts_loaded, 16)
                act.wait_ge(eps_ready, 1)
                nc.scalar.activation(root[:, :], eps[:, :], ACT.Sqrt)
                act.wait_ge(least_t_done, 1)
                nc.scalar.activation(least_row[0:1, 0:4 * P], part_ps[0][0:1, :], ACT.Copy)
                nc.scalar.activation(least_row[0:1, 4 * P:NCOL], part_ps[1][0:1, 0:NCOL - 4 * P], ACT.Copy).then_inc(least_row_ready, 1)
                banks = [ht_ps, hid1_ps, hid2_ps]
                for t in range(ROWT):
                    act.wait_ge(local_t_done, t + 1)
                    nc.scalar.activation(local_t[:, :, t * P:(t + 1) * P],
                                         banks[t % 3][:, 0:CHUNK].rearrange("p (j s) -> p j s", j=PER), ACT.Copy
                                         ).then_inc(local_t_ready, 1)

                def copy_part(q, par_q, rows=P):
                    act.wait_ge(seg_done, q + 1)
                    nc.scalar.activation(part[0:rows, par_q % 2, :], part_ps[par_q % 2][0:rows, 0:D], ACT.Copy
                                         ).then_inc(part_copied, 1)

                def x_sqrt(g):
                    rows, per = shape(g)
                    act.wait_ge(x_mv_ready, nth(g))
                    nc.scalar.activation(x_std[0:rows, 0:per], x_mv[0:rows, 0:per, 1], ACT.Sqrt, bias=eps[0:rows, 0:1]
                                         ).then_inc(x_std_ready, 1)

                def normalise(g):
                    rows, per = shape(g)
                    act.wait_ge(x_shift_ready, nth(g))
                    for j in range(per):
                        last = nc.scalar.activation(h[0:rows, j, :], xg(g, j), ACT.Relu, bias=x_shift[0:rows, j:j + 1],
                                                    scale=x_rstd[0:rows, j:j + 1])
                    last.then_inc(h_ready, 1)

                def copy_ht(g):
                    rows, per = shape(g)
                    act.wait_ge(h_transposed, nth(g))
                    t = h_t if rows == P else h_last_t
                    nc.scalar.activation(t[:, :].rearrange("f (p j) -> f j p", j=per),
                                         ht_ps[:, 0:rows * per].rearrange("f (j p) -> f j p", j=per), ACT.Copy
                                         ).then_inc(ht_ready, 1)

                def relu1(g):
                    n = shape(g)[0] * shape(g)[1]
                    act.wait_ge(hid1_done, g + 1)
                    nc.scalar.activation(hid1[:, 0:n], hid1_ps[:, 0:n], ACT.Relu, bias=b1s[:, 0:1]).then_inc(hid1_ready, 1)

                def relu2(g):
                    rows, per = shape(g)
                    act.wait_ge(hid2_done, g + 1)
                    nc.scalar.activation(hid2[:, 0:per, 0:rows], hid2_ps[:, 0:rows * per].rearrange("f (p j) -> f j p", j=per), ACT.Relu,
                                         bias=b2s[:, 0:1]).then_inc(hid2_ready, 1)

                def y_sqrt(g):
                    rows, per = shape(g)
                    act.wait_ge(y_mv_ready, g + 1)
                    nc.scalar.activation(y_std[0:rows, 0:per], y_mv[0:rows, 0:per, 1], ACT.Sqrt, bias=eps[0:rows, 0:1]
                                         ).then_inc(y_std_ready, 1)

                x_sqrt(LAST)
                normalise(LAST)
                copy_ht(LAST)

                def fast():
                    act.wait_ge(wts_loaded, 9 * 16)
                    x_sqrt(0)
                    normalise(0)
                    for q in range(AHEAD):
                        copy_part(q, q)
                    copy_ht(0)

                    def step(i, first=False, more_x=False):
                        q = 4 * i + AHEAD
                        copy_part(q, AHEAD)
                        relu1(i)
                        x_sqrt(i + 1)
                        copy_part(q + 1, AHEAD + 1)
                        relu2(i)
                        normalise(i + 1)
                        copy_part(q + 2, AHEAD + 2)
                        if not first:
                            y_sqrt(i - 1)
                        copy_part(q + 3, AHEAD + 3)
                        copy_ht(i + 1)
                        if more_x:
                            x_sqrt(i + 2)
                            normalise(i + 2)

                    step(0, first=True)
                    with act.Fori(1, STEPS - 2) as i:
                        step(i)
                    step(STEPS - 2, more_x=True)
                    q, g = QUADS - 4, GROUPS - 2
                    copy_part(q, q)
                    relu1(g)
                    copy_ht(g + 1)
                    copy_part(q + 1, q + 1)
                    relu2(g)
                    y_sqrt(g - 1)
                    copy_part(q + 2, q + 2)
                    copy_part(q + 3, q + 3)
                    relu1(g + 1)
                    y_sqrt(g)
                    copy_part(QUADS, QUADS, rows=WIN)
                    relu2(g + 1)
                    relu1(LAST)
                    relu2(LAST)
                    y_sqrt(g + 1)
                    act.wait_ge(y_centered, g + 2)
                    act.wait_ge(y_rstd_done, g + 2)
                    for j in range(PER):
                        nc.scalar.activation(z[:, j, :], z[:, j, :], ACT.Copy, scale=y_rstd[:, j:j + 1]).then_inc(z_scaled, 1)
                    y_sqrt(LAST)
                    act.wait_ge(full_out_ready, PER)
                    act.dma_start(group_rows(out, g + 1), xg(g + 1)).then_inc(stored, 16)

                def general():
                    act.wait_ge(wts_loaded, 9 * 16)

                    with act.Fori(0, GROUPS) as g:
                        x_sqrt(g)
                        normalise(g)
                        copy_ht(g)
                        relu1(g)
                        relu2(g)
                        y_sqrt(g)
                    relu1(LAST)
                    relu2(LAST)
                    y_sqrt(LAST)

                branch(act, fast, general)

            @block.gpsimd
            def _(pool):
                kw = dict(allow_small_or_imprecise_dtypes=True)
                nc.gpsimd.iota(iota[:, :], [[1, BANK]], base=0, channel_multiplier=0, **kw)
                nc.gpsimd.iota(pidx[:, :], [[0, 1]], base=0, channel_multiplier=1, **kw)
                nc.gpsimd.iota(turn[:, :], [[P * NODES_PER_CHUNK, ROWT]], base=-SLACK, channel_multiplier=NODES_PER_CHUNK,
                               **kw).then_inc(iotas_ready, 1)
                nc.gpsimd.memset(agg[:, :], 0.0).then_inc(agg_zeroed, 1)

                def rows_of(q, n, made):
                    if made:
                        pool.wait_ge(place_ready, q)
                    nc.gpsimd.tensor_copy(rows_at[:, 0:n], row_at[:, bass.ds(q, n)]).then_inc(rows_ready, 1)

                def placement(q, par_q, k, count, free=True):
                    if k == 0:
                        pool.wait_ge(rows_ready, count)
                    if free:
                        pool.wait_ge(placed, q - 1)
                        pool.sem_inc(pool_went_on, 1)
                    nc.gpsimd.tensor_scalar(place[:, par_q % 2, :], iota[:, 0:P], rows_at[:, k:k + 1], None,
                                            ALU.is_equal).then_inc(place_ready, 1)

                def bias_x(g):
                    rows, per = shape(g)
                    pool.wait_ge(h_ready, nth(g))
                    v = xg(g).rearrange("p (j f) -> p j f", j=per)
                    nc.gpsimd.tensor_tensor(v, v, lnbs[0:rows, :].unsqueeze(1).to_broadcast([rows, per, D]), ALU.add
                                            ).then_inc(x_biased, 1)

                pool.wait_ge(wts_loaded, 9 * 16)
                bias_x(LAST)

                def fast():
                    rows_of(0, AHEAD, False)
                    for q in range(2):
                        placement(q, q, q, 1, free=False)
                    bias_x(0)
                    for q in range(2, AHEAD):
                        placement(q, q, q, 1)

                    def step(i):
                        rows_of(4 * i + AHEAD, 4, True)
                        for k in range(4):
                            placement(4 * i + AHEAD + k, k, k, i + 2)
                        bias_x(i + 1)

                    with pool.Fori(0, STEPS) as i:
                        step(i)
                    rows_of(QUADS, 1, True)
                    placement(QUADS, QUADS, 0, STEPS + 2)
                    g = GROUPS - 1
                    pool.wait_ge(x_biased, nth(g))
                    for j in range(PER):
                        pool.wait_ge(z_scaled, j + 1)
                        nc.gpsimd.tensor_tensor(xg(g, j), z[:, j, :], xg(g, j), ALU.add).then_inc(full_out_ready, 1)

                def general():
                    with pool.Fori(0, GROUPS) as g:
                        bias_x(g)

                branch(pool, fast, general)

            @block.vector
            def _(dve):
                def stats_x(g, loaded, count):
                    rows, per = shape(g)
                    dve.wait_ge(loaded, count)
                    for j in range(per):
                        last = nc.vector.bn_stats(x_stats[0:rows, j, :], xg(g, j))
                    last.then_inc(x_stats_done, 1)

                def mean_x(g):
                    rows, per = shape(g)
                    dve.wait_ge(x_stats_done, nth(g))
                    dve.sem_inc(dve_went_on, 1)
                    for j in range(per):
                        last = nc.vector.bn_aggr(x_mv[0:rows, j, :], x_stats[0:rows, j, :])
                    last.then_inc(x_mv_ready, 1)

                def scale_x(g):
                    rows, per = shape(g)
                    dve.wait_ge(x_std_ready, nth(g))
                    nc.vector.reciprocal(x_rstd[0:rows, 0:per], x_std[0:rows, 0:per]).then_inc(x_rstd_done, 1)

                def shift_x(g):
                    rows, per = shape(g)
                    dve.wait_ge(x_rstd_done, nth(g))
                    nc.vector.scalar_tensor_tensor(x_shift[0:rows, 0:per], x_mv[0:rows, 0:per, 0], -1.0, x_rstd[0:rows, 0:per],
                                                   ALU.mult, ALU.mult).then_inc(x_shift_ready, 1)

                nc.vector.memset(dst_i[:, ROWT - 1, :], 0).then_inc(dst_padded, 1)
                nc.vector.memset(base_i[:, :], 0)
                nc.vector.memset(eps[:, :], EPS).then_inc(eps_ready, 1)
                nc.vector.memset(signs[0:1, 0, :], 1.0)
                nc.vector.memset(signs[0:1, 1, :], -1.0)
                nc.vector.memset(excess[:, :], -1.0)
                dve.wait_ge(iotas_ready, 1)
                nc.vector.tensor_scalar(ident[:, :], iota[:, 0:P], pidx[:, 0:1], None, ALU.is_equal).then_inc(ident_ready, 1)
                for s in range(QC):
                    rows = slice(s * WIN, (s + 1) * WIN)
                    nc.vector.tensor_scalar(widx[rows, :], pidx[rows, :], float(s * WIN), None, ALU.subtract)
                dve.wait_ge(dst_loaded, 3 * 16)
                nc.vector.tensor_reduce(least[:, :], dst_i[:, :, :], AX.X, ALU.min).then_inc(least_ready, 1)
                dve.wait_ge(least_ready, 1)
                nc.vector.tensor_tensor(local3, dst_i[:, :, :], least[:, :].unsqueeze(2).to_broadcast([P, ROWT, CHUNK]),
                                        ALU.subtract).then_inc(local_ready, 1)
                dve.wait_ge(local_ready, 1)
                nc.vector.tensor_reduce(span[:, :], local3, AX.X, ALU.max)
                nc.vector.tensor_tensor(turn[:, :], turn[:, :], least[:, :], ALU.subtract).then_inc(span_ready, 1)
                dve.wait_ge(least_row_ready, 1)
                nc.vector.tensor_copy(base_i[0:1, 3:3 + QUADS + 1], least_row[0:1, 0:4 * QUADS + 1:QC]).then_inc(base_ready, 1)
                stats_x(LAST, last_x_loaded, 16 * len(LAST_PARTS))
                mean_x(LAST)
                dve.wait_ge(row_at_done, 1)
                nc.vector.tensor_scalar(row_at[:, :], place_ps[0][:, 0:QUADS + 1], widx[:, 0:1], None, ALU.add).then_inc(row_at_ready, 1)
                dve.wait_ge(span_ready, 1)
                dve.wait_ge(row_at_ready, 1)
                nc.vector.tensor_reduce(excess[:, 0:1], span[:, :], AX.X, ALU.max)
                nc.vector.tensor_reduce(excess[:, 1:2], row_at[:, 0:QUADS], AX.X, ALU.max)
                nc.vector.tensor_reduce(excess[:, 2:3], row_at[:, 0:QUADS], AX.X, ALU.min)
                nc.vector.tensor_reduce(excess[:, 3:4], turn[:, 0:ROWT - 1], AX.X, ALU.max)
                nc.vector.tensor_copy(excess[0:LROW + 1, 4:5], turn[0:LROW + 1, ROWT - 1:ROWT]).then_inc(span_ready, 1)
                dve.wait_ge(span_ready, 2)
                nc.vector.tensor_scalar(excess[:, 0:1], excess[:, 0:1], float(WIN - 1), None, ALU.subtract)
                nc.vector.tensor_scalar(excess[:, 1:2], excess[:, 1:2], float(P - 1), None, ALU.subtract)
                nc.vector.tensor_scalar(excess[:, 2:3], excess[:, 2:3], -1.0, None, ALU.mult).then_inc(span_ready, 1)
                dve.wait_ge(span_ready, 3)
                nc.vector.tensor_reduce(excess1[:, 0:1], excess[:, :], AX.X, ALU.max).then_inc(excess_ready, 1)
                scale_x(LAST)
                shift_x(LAST)
                dve.wait_ge(local_t_ready, ROWT)
                whole = DONE // PER
                nc.vector.memset(local_t[0:whole, DONE % PER:PER, CHUNKS:CHUNKS + 1], -1.0)
                nc.vector.memset(local_t[0:whole + 1, 0:DONE % PER, CHUNKS:CHUNKS + 1], -1.0).then_inc(tail_masked, 1)
                dve.wait_ge(excess_t_done, 1)
                nc.vector.tensor_reduce(worst[:, :], place_ps[1][0:1, 0:P], AX.X, ALU.max).then_inc(worst_ready, 1)
                dve.wait_ge(worst_ready, 1)
                nc.vector.tensor_scalar(flag_i[:, :], worst[:, :], 0.0, None, ALU.is_le).then_inc(flag_ready, 1)

                def make_onehot(m, par, free=True):
                    if free:
                        dve.wait_ge(seg_done, 2 * m - 2)
                    nc.vector.tensor_tensor(
                        onehot[:, par % 2, :, :, :],
                        iota[:, 0:WIN].unsqueeze(1).unsqueeze(1).to_broadcast([P, OCT, PER, WIN]),
                        local_t[:, :, bass.ds(m * OCT, OCT)].rearrange("p j s -> p s j").unsqueeze(3).to_broadcast([P, OCT, PER, WIN]),
                        ALU.is_equal).then_inc(onehot_ready, 1)

                def bases(q0, n):
                    _, values = nc.values_load_multi_w_load_instructions(
                        base_i[0:1, bass.ds(q0 + 3, n)], engines=[mybir.EngineType.DVE], min_val=0, max_val=AGG - P,
                        skip_runtime_bounds_check_because="the least of dst, which names a node")
                    return values

                def add(q, par_q, base):
                    dve.wait_ge(placed, q + 1)
                    if not (isinstance(q, int) and q == 0):
                        dve.wait_ge(added, q)
                    v = agg[:, bass.ds(base, P)]
                    nc.vector.tensor_tensor(v, place_ps[par_q % 2][:, 0:P], v, ALU.add).then_inc(added, 1)

                def take_y(g):
                    dve.wait_ge(y_done, g + 1)
                    nc.vector.tensor_tensor(y[:, :, :], y_ps[:, 0:CHUNK].rearrange("p (j f) -> p j f", j=PER),
                                            b3s[:, :].unsqueeze(1).to_broadcast([P, PER, D]), ALU.add).then_inc(y_evacuated, 1)

                def z_of(g, j):
                    rows, per = shape(g)
                    return z[:, j, :] if rows == P else y[0:rows, j, :]

                def y_of(g, j):
                    rows, per = shape(g)
                    return y[:, j, :] if rows == P else y_last_ps[0:rows, j * D:(j + 1) * D]

                def stats_y(g):
                    rows, per = shape(g)
                    if rows == P:
                        dve.wait_ge(y_evacuated, g + 1)
                    else:
                        dve.wait_ge(y_done, g + 1)
                    for j in range(per):
                        last = nc.vector.bn_stats(y_stats[0:rows, j, :], y_of(g, j))
                    last.then_inc(y_stats_done, 1)

                def mean_y(g):
                    rows, per = shape(g)
                    dve.wait_ge(y_stats_done, g + 1)
                    dve.sem_inc(dve_went_on, 1)
                    for j in range(per):
                        last = nc.vector.bn_aggr(y_mv[0:rows, j, :], y_stats[0:rows, j, :])
                    last.then_inc(y_mv_ready, 1)

                def center_y(g):
                    rows, per = shape(g)
                    dve.wait_ge(y_mv_ready, g + 1)
                    for j in range(per):
                        last = nc.vector.scalar_tensor_tensor(z_of(g, j), y_of(g, j), y_mv[0:rows, j, 0:1], lnws[0:rows, :],
                                                              ALU.subtract, ALU.mult)
                    last.then_inc(y_centered, 1)

                def scale_y(g):
                    rows, per = shape(g)
                    dve.wait_ge(y_std_ready, g + 1)
                    r = y_rstd if rows == P else y_last_rstd
                    nc.vector.reciprocal(r[0:rows, 0:per], y_std[0:rows, 0:per]).then_inc(y_rstd_done, 1)

                def output(g):
                    rows, per = shape(g)
                    dve.wait_ge(y_rstd_done, g + 1)
                    dve.wait_ge(y_centered, g + 1)
                    dve.wait_ge(x_biased, nth(g))
                    r = y_rstd if rows == P else y_last_rstd
                    for j in range(per):
                        last = nc.vector.scalar_tensor_tensor(xg(g, j), z_of(g, j), r[0:rows, j:j + 1], xg(g, j),
                                                              ALU.mult, ALU.add)
                    last.then_inc(out_ready, 1)

                def finish(g):
                    if shape(g)[0] == P:
                        take_y(g)
                    stats_y(g)
                    mean_y(g)
                    center_y(g)
                    scale_y(g)
                    output(g)

                def fast():
                    dve.wait_ge(tail_masked, 1)
                    dve.wait_ge(wts_loaded, 9 * 16)
                    make_onehot(0, 0, free=False)
                    make_onehot(1, 1, free=False)
                    stats_x(0, x_loaded[0], 16)
                    mean_x(0)
                    scale_x(0)
                    shift_x(0)
                    dve.wait_ge(base_ready, 1)
                    dve.wait_ge(agg_zeroed, 1)
                    base = bases(0, AHEAD - 1)
                    add(0, 0, base[0])
                    make_onehot(2, 2)
                    add(1, 1, base[1])
                    add(2, 2, base[2])
                    make_onehot(3, 3)
                    add(3, 3, base[3])
                    add(4, 4, base[4])

                    def step(i, par, pairs, first=False, more_x=False):
                        make_onehot(2 * i + 4, 0)
                        base = bases(4 * i + AHEAD - 1, 4)
                        q = 4 * i + AHEAD - 1
                        add(q, 1, base[0])
                        stats_x(i + 1, x_loaded[1 - par], 16 * (pairs + par) + 16)
                        if not first:
                            take_y(i - 1)
                        add(q + 1, 0, base[1])
                        mean_x(i + 1)
                        if not first:
                            stats_y(i - 1)
                        scale_x(i + 1)
                        shift_x(i + 1)
                        if not first:
                            mean_y(i - 1)
                        add(q + 2, 1, base[2])
                        if not first:
                            center_y(i - 1)
                        make_onehot(2 * i + 5, 1)
                        if more_x:
                            stats_x(i + 2, x_loaded[par], 16 * pairs + 32)
                            mean_x(i + 2)
                        add(q + 3, 0, base[3])
                        if more_x:
                            scale_x(i + 2)
                            shift_x(i + 2)
                        if not first:
                            scale_y(i - 1)
                            output(i - 1)

                    step(0, 0, 0, first=True)
                    with dve.Fori(0, (STEPS - 3) // 2) as t:
                        step(2 * t + 1, 1, t)
                        step(2 * t + 2, 0, t + 1)
                    step(STEPS - 2, 1, (STEPS - 2) // 2, more_x=True)
                    q, g = QUADS - 4, GROUPS - 2
                    make_onehot(q // 2 + 1, 0)
                    base = bases(q - 1, 3) + bases(q + 2, 3)
                    take_y(g - 1)
                    add(q - 1, q - 1, base[0])
                    stats_y(g - 1)
                    mean_y(g - 1)
                    add(q, q, base[1])
                    center_y(g - 1)
                    make_onehot(q // 2 + 2, 1)
                    add(q + 1, q + 1, base[2])
                    scale_y(g - 1)
                    output(g - 1)
                    add(q + 2, q + 2, base[3])
                    take_y(g)
                    stats_y(g)
                    mean_y(g)
                    center_y(g)
                    scale_y(g)
                    add(q + 3, q + 3, base[4])
                    output(g)
                    add(QUADS, QUADS, base[5])
                    take_y(g + 1)
                    stats_y(g + 1)
                    mean_y(g + 1)
                    center_y(g + 1)
                    scale_y(g + 1)
                    finish(LAST)

                def general():
                    d2 = dst_i[:, :, :].rearrange("p t k -> p (t k)")
                    cols = BLOCKS * BLOCK + RC
                    dve.wait_ge(tail_masked, 1)
                    dve.wait_ge(agg_zeroed, 1)
                    dve.wait_ge(wts_loaded, 9 * 16)
                    for k in range(RING):
                        dve.wait_ge(edges_loaded[k], 16)
                    nc.vector.memset(place[:, 0, :], 0.0).then_inc(zeros_ready, 1)
                    nc.vector.memset(local[RP:P, BLOCKS * BLOCK:BLOCKS * BLOCK + RC], -1.0)
                    dve.wait_ge(dst2_loaded, 32)
                    nc.vector.tensor_copy(local[:, 0:BLOCKS * BLOCK], d2[:, 0:BLOCKS * BLOCK])
                    nc.vector.tensor_copy(local[0:RP, BLOCKS * BLOCK:cols], d2[0:RP, BLOCKS * BLOCK:cols]).then_inc(dst2_ready, 1)
                    dve.sem_inc(block_done, 2)
                    dve.sem_inc(dense_used, 2)
                    dve.sem_inc(window_free, 1)

                    def dense(col, n, par, count, rows=P):
                        dve.wait_ge(dense_used, count)
                        for c in range(n):
                            last = nc.vector.tensor_scalar(ring[0:rows, 2 + par, c * BANK:(c + 1) * BANK], iota[0:rows, :],
                                                           local[0:rows, bass.ds(col + c, 1)], None, ALU.is_equal)
                        last.then_inc(dense_ready, 1)

                    with dve.Fori(0, WINDOWS) as w:
                        dve.wait_ge(dst2_ready, w + 1)
                        dve.sem_inc(dve_went_on, 1)
                        with dve.Fori(0, BLOCKS) as b:
                            for k in range(BLOCK // 3):
                                dense(b * BLOCK + 3 * k, 3, k % 2, w * TRIPLES + b * (BLOCK // 3) + k + 1)
                        dense(BLOCKS * BLOCK, 3, 0, w * TRIPLES + TRIPLES - 1, RP)
                        dense(BLOCKS * BLOCK + 3, RC - 3, 1, w * TRIPLES + TRIPLES, RP)
                        dve.wait_ge(dense_ready, w * TRIPLES + TRIPLES)
                        nc.vector.tensor_scalar(local[:, 0:cols], local[:, 0:cols], float(BANK), None, ALU.subtract).then_inc(dst2_ready, 1)
                        dve.wait_ge(window_done, w + 1)
                        nc.vector.tensor_copy(agg[:, bass.ds(w * BANK, BANK)], part_ps[0][:, :]).then_inc(window_free, 1)

                    def group(g, par, pairs):
                        stats_x(g, x_loaded[par], 16 * pairs + 16)
                        mean_x(g)
                        scale_x(g)
                        shift_x(g)
                        finish(g)

                    with dve.Fori(0, GROUPS // 2) as t:
                        group(2 * t, 0, t)
                        group(2 * t + 1, 1, t)
                    finish(LAST)

                branch(dve, fast, general)


_INS = ["x", "dst", "edge_attr_128", "L0_gnn_W1", "L0_gnn_b1", "L0_gnn_W2", "L0_gnn_b2", "L0_gnn_W3", "L0_gnn_b3",
        "L0_gnn_ln_w", "L0_gnn_ln_b"]


def kernel(**inputs):
    import concourse.bacc as bacc
    from concourse.bass_utils import run_bass_kernel_spmd

    nc = bacc.Bacc("TRN2", target_bir_lowering=False, num_devices=1)
    arrays, args = {}, []
    for name in _INS:
        a = np.ascontiguousarray(inputs[name])
        arrays[f"in_{name}"] = a
        args.append(nc.dram_tensor(f"in_{name}", a.shape, mybir.dt.from_np(a.dtype), kind="ExternalInput").ap())
    args.append(nc.dram_tensor("out_x", (NODES, D), F32, kind="ExternalOutput").ap())
    gnn_kernel(nc, *args)
    r = run_bass_kernel_spmd(nc, [arrays], core_ids=[0])
    return r.results[0]["out_x"]
```
